# Optimizing a Trainium2 kernel written in Bass

```python
import numpy as np
import jax
import jax.numpy as jnp

def _softmax(x, axis=-1):
    return jax.nn.softmax(x, axis=axis)

def _gelu(x):
    return jax.nn.gelu(x, approximate=True)

def _silu(x):
    return jax.nn.silu(x)

def _sigmoid(x):
    return jax.nn.sigmoid(x)

def _layernorm(x, axis=-1, eps=1e-05):
    m = jnp.mean(x, axis=axis, keepdims=True)
    v = jnp.var(x, axis=axis, keepdims=True)
    return (x - m) / jnp.sqrt(v + eps)

def _scatter_add(tgt, idx, src, axis=0):
    return tgt.at[idx].add(src)

def _segment_sum(src, seg, n):
    return jax.ops.segment_sum(src, seg, n)
kernel_name = 'mk_decoder_postln_d1_seqx_r8_b57969'

def setup_inputs(seed: int=0):
    np.random.seed(seed)
    _w = jnp.asarray

    def _rec_inputs():
        import jax
        import jax.numpy as jnp
        _rk = jax.random.key(seed)
        x = -0.0003929 + 0.9999 * jax.random.normal(jax.random.fold_in(_rk, 1), (2, 512, 128), jnp.float32)
        _lenS = 512 - jax.random.randint(jax.random.fold_in(_rk, 7), (2,), 0, max(1, 512 // 4) + 1, jnp.int32)
        _lenS2 = 77 - jax.random.randint(jax.random.fold_in(_rk, 8), (2,), 0, max(1, 77 // 4) + 1, jnp.int32)
        _ctx_1024P = jax.random.normal(jax.random.fold_in(_rk, 11), (2, 16, 128), jnp.float32)
        _ctx_1024c = jax.random.dirichlet(jax.random.fold_in(_rk, 511), 0.3 * jnp.ones((16,), jnp.float32), (2, 77))
        _ctx_1024t = jnp.einsum('bsk,bkd->bsd', _ctx_1024c, _ctx_1024P)
        _ctx_1024t = _ctx_1024t * jax.lax.rsqrt(jnp.mean(jnp.square(_ctx_1024t)) + 1e-12) * 0.953939
        ctx_1024 = 2.81802e-05 + 1.00001 * (_ctx_1024t + 0.3 * jax.random.normal(jax.random.fold_in(_rk, 611), (2, 77, 128), jnp.float32))
        _validS = jnp.arange(512)[None, :] < _lenS[:, None]
        _validS2 = jnp.arange(77)[None, :] < _lenS2[:, None]
        _causal = jnp.tril(jnp.ones((512, 512), dtype=bool))
        mask_BxS2_if1 = jnp.where(jnp.ones((2, 77), dtype=bool), 1, 0).astype(jnp.int32)
        return (x, ctx_1024, mask_BxS2_if1)
    x, ctx_1024, mask_BxS2_if1 = _rec_inputs()

    def _L0_attn_setup():
        import jax, jax.numpy as jnp
        import numpy as np
        from math import log2, floor
        HEADS = 16
        DIM_HEAD = 64
        SCALE = DIM_HEAD ** (-0.5)

        def _get_slopes(heads):

            def pow2_slopes(n):
                start = 2 ** (-2 ** (-(log2(n) - 3)))
                return [start * start ** i for i in range(n)]
            if log2(heads).is_integer():
                return pow2_slopes(heads)
            c = 2 ** floor(log2(heads))
            return pow2_slopes(c) + pow2_slopes(2 * c)[0::2][:heads - c]
        key = jax.random.key(seed)
        k1, k2, k3 = jax.random.split(key, 3)
        b, n, dim = (2, 256, 128)
        inner = HEADS * DIM_HEAD
        x = jax.random.normal(k1, (b, n, dim), dtype=jnp.float32)
        w_qkv = jax.random.normal(k2, (dim, 3 * inner), dtype=jnp.float32) * dim ** (-0.5)
        w_out = jax.random.normal(k3, (inner, dim), dtype=jnp.float32) * inner ** (-0.5)
        b_out = jnp.zeros((dim,), dtype=jnp.float32)
        return {'x': x, 'w_qkv': w_qkv, 'w_out': w_out, 'b_out': b_out}
    _L0_attn_all = _L0_attn_setup()
    _L0_attn_in = {k: v for k, v in _L0_attn_all.items() if k in ('w_qkv', 'w_out', 'b_out')}
    del _L0_attn_all

    def _L0_xattn_setup():
        import jax, jax.numpy as jnp
        import numpy as np
        key = jax.random.key(seed)
        ks = jax.random.split(key, 9)
        B, T, D = (4, 512, 128)
        scale = 1.0 / np.sqrt(D)
        inp = {'q': jax.random.normal(ks[0], (B, T, D), dtype=jnp.float32), 'k': jax.random.normal(ks[1], (B, T, D), dtype=jnp.float32), 'v': jax.random.normal(ks[2], (B, T, D), dtype=jnp.float32), 'Wq': jax.random.normal(ks[3], (D, D), dtype=jnp.float32) * scale, 'bq': jnp.zeros((D,), dtype=jnp.float32), 'Wk': jax.random.normal(ks[4], (D, D), dtype=jnp.float32) * scale, 'bk': jnp.zeros((D,), dtype=jnp.float32), 'Wv': jax.random.normal(ks[5], (D, D), dtype=jnp.float32) * scale, 'bv': jnp.zeros((D,), dtype=jnp.float32), 'mask': jnp.ones((B, T), dtype=jnp.int32)}
        return inp
    _L0_xattn_all = _L0_xattn_setup()
    _L0_xattn_in = {k: v for k, v in _L0_xattn_all.items() if k in ('Wq', 'bq', 'Wk', 'bk', 'Wv', 'bv')}
    del _L0_xattn_all

    def _L0_ffn_setup():
        import jax, jax.numpy as jnp
        import numpy as np
        B, T, C = (2, 128, 128)
        H = 512
        E_R, E_S, K = (8, 2, 2)

        def _rmsnorm(x, g):
            eps = jnp.finfo(x.dtype).eps
            return x * jax.lax.rsqrt(jnp.mean(x * x, axis=-1, keepdims=True) + eps) * g

        def _experts_mlp(x, g, W1, b1, W2, b2):
            xn = _rmsnorm(x, g)
            h = jnp.einsum('btc,ech->bteh', xn, W1) + b1
            h = jax.nn.gelu(h, approximate=False)
            return jnp.einsum('bteh,ehc->btec', h, W2) + b2
        key = jax.random.key(seed)
        ks = jax.random.split(key, 12)
        s = 0.02
        return {'u': jax.random.normal(ks[0], (B, T, C), dtype=jnp.float32), 'g_shared': jnp.ones((C,), jnp.float32), 'W1_s': jax.random.normal(ks[1], (E_S, C, H), jnp.float32) * s, 'b1_s': jax.random.normal(ks[2], (E_S, H), jnp.float32) * s, 'W2_s': jax.random.normal(ks[3], (E_S, H, C), jnp.float32) * s, 'b2_s': jax.random.normal(ks[4], (E_S, C), jnp.float32) * s, 'g_routed': jnp.ones((C,), jnp.float32), 'W1_r': jax.random.normal(ks[5], (E_R, C, H), jnp.float32) * s, 'b1_r': jax.random.normal(ks[6], (E_R, H), jnp.float32) * s, 'W2_r': jax.random.normal(ks[7], (E_R, H, C), jnp.float32) * s, 'b2_r': jax.random.normal(ks[8], (E_R, C), jnp.float32) * s, 'centroids': jax.random.normal(ks[9], (C, E_R), jnp.float32) * s}
    _L0_ffn_all = _L0_ffn_setup()
    _L0_ffn_in = {k: v for k, v in _L0_ffn_all.items() if k in ('g_shared', 'W1_s', 'b1_s', 'W2_s', 'b2_s', 'g_routed', 'W1_r', 'b1_r', 'W2_r', 'b2_r', 'centroids')}
    del _L0_ffn_all
    return {'x': x, 'ctx_1024': ctx_1024, 'mask_BxS2_if1': mask_BxS2_if1, 'L0_attn_w_qkv': _L0_attn_in['w_qkv'], 'L0_attn_w_out': _L0_attn_in['w_out'], 'L0_attn_b_out': _L0_attn_in['b_out'], 'L0_xattn_Wq': _L0_xattn_in['Wq'], 'L0_xattn_bq': _L0_xattn_in['bq'], 'L0_xattn_Wk': _L0_xattn_in['Wk'], 'L0_xattn_bk': _L0_xattn_in['bk'], 'L0_xattn_Wv': _L0_xattn_in['Wv'], 'L0_xattn_bv': _L0_xattn_in['bv'], 'L0_ffn_g_shared': _L0_ffn_in['g_shared'], 'L0_ffn_W1_s': _L0_ffn_in['W1_s'], 'L0_ffn_b1_s': _L0_ffn_in['b1_s'], 'L0_ffn_W2_s': _L0_ffn_in['W2_s'], 'L0_ffn_b2_s': _L0_ffn_in['b2_s'], 'L0_ffn_g_routed': _L0_ffn_in['g_routed'], 'L0_ffn_W1_r': _L0_ffn_in['W1_r'], 'L0_ffn_b1_r': _L0_ffn_in['b1_r'], 'L0_ffn_W2_r': _L0_ffn_in['W2_r'], 'L0_ffn_b2_r': _L0_ffn_in['b2_r'], 'L0_ffn_centroids': _L0_ffn_in['centroids']}

def reference(x, ctx_1024, mask_BxS2_if1, L0_attn_w_qkv, L0_attn_w_out, L0_attn_b_out, L0_xattn_Wq, L0_xattn_bq, L0_xattn_Wk, L0_xattn_bk, L0_xattn_Wv, L0_xattn_bv, L0_ffn_g_shared, L0_ffn_W1_s, L0_ffn_b1_s, L0_ffn_W2_s, L0_ffn_b2_s, L0_ffn_g_routed, L0_ffn_W1_r, L0_ffn_b1_r, L0_ffn_W2_r, L0_ffn_b2_r, L0_ffn_centroids):
    import jax
    import jax.numpy as jnp

    def _L0_attn_ref(x, w_qkv, w_out, b_out):
        import jax, jax.numpy as jnp
        import numpy as np
        from math import log2, floor
        HEADS = 16
        DIM_HEAD = 64
        SCALE = DIM_HEAD ** (-0.5)

        def _get_slopes(heads):

            def pow2_slopes(n):
                start = 2 ** (-2 ** (-(log2(n) - 3)))
                return [start * start ** i for i in range(n)]
            if log2(heads).is_integer():
                return pow2_slopes(heads)
            c = 2 ** floor(log2(heads))
            return pow2_slopes(c) + pow2_slopes(2 * c)[0::2][:heads - c]
        b, n, _ = x.shape
        qkv = x @ w_qkv
        q, k, v = jnp.split(qkv, 3, axis=-1)

        def to_heads(t):
            return t.reshape(b, n, HEADS, DIM_HEAD).transpose(0, 2, 1, 3)
        q, k, v = map(to_heads, (q, k, v))
        q = q * SCALE
        sim = jnp.einsum('bhid,bhjd->bhij', q, k)
        slopes = jnp.asarray(_get_slopes(HEADS), dtype=sim.dtype)[:, None, None]
        i = jnp.arange(n)
        rel = -jnp.abs(i[None, :] - i[:, None]).astype(sim.dtype)
        sim = sim + rel[None, :, :] * slopes
        causal = jnp.triu(jnp.ones((n, n), dtype=bool), 1)
        mask_value = -jnp.finfo(sim.dtype).max
        sim = jnp.where(causal, mask_value, sim)
        attn = jax.nn.softmax(sim, axis=-1)
        out = jnp.einsum('bhij,bhjd->bhid', attn, v)
        out = out.transpose(0, 2, 1, 3).reshape(b, n, HEADS * DIM_HEAD)
        return out @ w_out + b_out

    def _L0_xattn_ref(q, k, v, Wq, bq, Wk, bk, Wv, bv, mask):
        import jax, jax.numpy as jnp
        import numpy as np
        query = jnp.einsum('btd,de->bte', q, Wq) + bq
        key_ = jnp.einsum('bsd,de->bse', k, Wk) + bk
        value = jnp.einsum('bsd,de->bse', v, Wv) + bv
        dim_k = key_.shape[-1]
        scores = jnp.einsum('bte,bse->bts', query, key_) / jnp.sqrt(jnp.asarray(dim_k, dtype=query.dtype))
        scores = jnp.where(mask[:, None, :] == 0, -jnp.inf, scores)
        weights = jax.nn.softmax(scores, axis=-1)
        outputs = jnp.einsum('bts,bse->bte', weights, value)
        return outputs

    def _L0_ffn_ref(u, g_shared, W1_s, b1_s, W2_s, b2_s, g_routed, W1_r, b1_r, W2_r, b2_r, centroids):
        import jax, jax.numpy as jnp
        import numpy as np
        B, T, C = (2, 128, 128)
        H = 512
        E_R, E_S, K = (8, 2, 2)

        def _rmsnorm(x, g):
            eps = jnp.finfo(x.dtype).eps
            return x * jax.lax.rsqrt(jnp.mean(x * x, axis=-1, keepdims=True) + eps) * g

        def _experts_mlp(x, g, W1, b1, W2, b2):
            xn = _rmsnorm(x, g)
            h = jnp.einsum('btc,ech->bteh', xn, W1) + b1
            h = jax.nn.gelu(h, approximate=False)
            return jnp.einsum('bteh,ehc->btec', h, W2) + b2
        h_s = _experts_mlp(u, g_shared, W1_s, b1_s, W2_s, b2_s).sum(axis=-2)
        scores = jax.nn.sigmoid(u @ centroids)
        gpk, i_topk = jax.lax.top_k(scores, K)
        gk = gpk / scores.sum(axis=-1, keepdims=True)
        routed_all = _experts_mlp(u, g_routed, W1_r, b1_r, W2_r, b2_r)
        routed_topk = jnp.take_along_axis(routed_all, i_topk[..., None], axis=2)
        h_r = (gk[..., None] * routed_topk).sum(axis=-2)
        return u + h_s + h_r
    x = _layernorm(x + _L0_attn_ref(x, L0_attn_w_qkv, L0_attn_w_out, L0_attn_b_out), axis=-1)
    x = _layernorm(x + _L0_xattn_ref(x, ctx_1024, ctx_1024, L0_xattn_Wq, L0_xattn_bq, L0_xattn_Wk, L0_xattn_bk, L0_xattn_Wv, L0_xattn_bv, mask_BxS2_if1), axis=-1)
    x = _layernorm(x + _L0_ffn_ref(x, L0_ffn_g_shared, L0_ffn_W1_s, L0_ffn_b1_s, L0_ffn_W2_s, L0_ffn_b2_s, L0_ffn_g_routed, L0_ffn_W1_r, L0_ffn_b1_r, L0_ffn_W2_r, L0_ffn_b2_r, L0_ffn_centroids), axis=-1)
    return x

_drawn_inputs = setup_inputs


def setup_inputs(seed=0):
    import zlib

    import numpy as np

    out = dict(_drawn_inputs(seed))
    spreads = {'L0_attn_b_out': (0.0, 0.1),
     'L0_xattn_bq': (0.0, 0.303),
     'L0_xattn_bk': (0.0, 2.0),
     'L0_xattn_bv': (0.0, 0.1),
     'L0_ffn_g_shared': (1.0, 0.6),
     'L0_ffn_g_routed': (1.0, 0.6)}
    factors = {'L0_ffn_b1_s': 22.068,
     'L0_ffn_b2_s': 4.129,
     'L0_ffn_W1_r': 8.0,
     'L0_ffn_b1_r': 8.0,
     'L0_ffn_W2_r': 8.0,
     'L0_ffn_b2_r': 25.769,
     'L0_ffn_centroids': 8.0}
    for name, (base, spread) in spreads.items():
        noise = np.random.default_rng([zlib.crc32(name.encode()), seed]).standard_normal(out[name].shape)
        drawn = base * np.exp(spread * noise) if base else spread * noise
        out[name] = jnp.asarray(drawn.astype(out[name].dtype))
    for name, factor in factors.items():
        out[name] = (out[name] * factor).astype(out[name].dtype)
    return out
```

```python
import concourse.bass as bass
from concourse import mybir
from contextlib import ExitStack

F32 = mybir.dt.float32
F32R = mybir.dt.float32r
I32 = mybir.dt.int32
ALU = mybir.AluOpType
ACT = mybir.ActivationFunctionType
AXIS = mybir.AxisListType

B, N, C = 2, 512, 128
HEADS, DH = 16, 64
S2 = 77
HID, ES, ER = 512, 2, 8
P = 128
NT = N // P
PAIRS = HEADS // 2
UNITS = B * PAIRS
KC = HID // P
E = ES + ER
CHUNKS = E * KC
SCALE = DH ** -0.5
XSCALE = float(C) ** -0.5
LN_EPS = 1e-5
RMS_EPS = 1.1920928955078125e-07
NEG = 1e30
BIG = 3e38
SLOPES = [(2.0 ** (-2.0 ** (-(4 - 3)))) ** (h + 1) for h in range(HEADS)]
BANKS = 6
ROW_AT = [sum(P * (k + 1) for k in range(i)) for i in range(NT)]
HEAD_COLS = ROW_AT[-1] + P * NT
GROUPS = [[0], [1, 3], [2]]
GROUP_AT = [0, 512, 1024]
KEY_AT = [0, 512, 1024, 896]
FFN_SLOTS = 3
LAG = 3


def build_schedule():
    s = []

    def scores(u, i):
        s.append(("score", (u, i, 0)))
        s.append(("score", (u, i, 1)))

    def chain(b):
        return [("yT", (b,)), ("res1", (b,)), ("x1", (b,)), ("x1T", (b,)), ("xq", (b,)), ("xscore", (b,)),
                ("xprob", (b,)), ("xpT", (b,)), ("xout", (b,)), ("x2", (b,)), ("x2T", (b,)), ("xr", (b,)),
                ("logit", (b,)), ("gates", (b,)), ("gatesT", (b,)), ("xnT", (b,))]

    s.append(("xT", (0,)))
    s.append(("projQ", (0,)))
    s.append(("projK", (0,)))
    s.append(("xT", (1,)))
    waiting = []
    for u in range(UNITS + 1):
        now, before, after = u < UNITS, u >= 1, u + 1 < UNITS
        if u == 9:
            waiting = chain(0)
        seg = [[] for _ in range(12)]

        def link(k):
            for _ in range(k):
                if waiting and (u < 15 or waiting[0][0] != "xnT"):
                    s.append(waiting.pop(0))
        if now:
            scores(u, 0)
        if before:
            s.append(("norm", (u - 1, NT - 1)))
        if u >= 2:
            s.append(("outproj", (u - 2, 1)))
        if after:
            s.append(("projQ", (u + 1,)))
        if now:
            scores(u, 1)
            s.append(("norm", (u, 0)))
        if after:
            s.append(("projK", (u + 1,)))
        if u == 0:
            s.append(("cols", ()))
            s.append(("split_wout", ()))
            s += [("V", (0, 0, t)) for t in range(NT)]
        if u == 1:
            s += [("V", (0, 1, t)) for t in range(NT)]
            s.append(("ctxT", ()))
            s.append(("ctxK", ()))
            s.append(("ctxV", ()))
        link(1)
        if before:
            s.append(("probT", (u - 1, 0, 0)))
            s.append(("probT", (u - 1, 0, 1)))
            s.append(("probT", (u - 1, 0, 2)))
        if now:
            scores(u, 2)
            s.append(("norm", (u, 1)))
        link(1)
        if before:
            s.append(("probT", (u - 1, 1, 0)))
            s.append(("attn", (u - 1, 0)))
            s.append(("probT", (u - 1, 1, 1)))
            s.append(("probT", (u - 1, 1, 2)))
        if now:
            scores(u, 3)
            s.append(("norm", (u, 2)))
        link(1)
        if before:
            s.append(("outproj", (u - 1, 0)))
            s.append(("attn", (u - 1, 1)))
        if u == 7:
            pass
        if u == 5:
            s += [("V", (1, 0, t)) for t in range(NT)]
        if u == 9:
            s += [("V", (1, 1, t)) for t in range(NT)]
        if u == 14:
            s += [("split_ffn", (0,)), ("split_ffn", (1,))]
        if u == 15:
            s.append(("split_ffn", (2,)))
    s.append(("outproj", (UNITS - 1, 1)))
    s += waiting
    for b in range(B):
        waiting = chain(1) if b == 0 else []
        for c in range(CHUNKS + LAG):
            e, k = divmod(c, KC)
            if c < CHUNKS:
                if k == 0 and e >= ES:
                    s.append(("gate_b", (b, e)))
                if k == LAG and FFN_SLOTS <= b * E + e + 2 < B * E:
                    s.append(("split_ffn", (b * E + e + 2,)))
                s.append(("up", (b, c)))
            if c >= LAG:
                s.append(("down", (b, c - LAG)))
                e2, k2 = divmod(c - LAG, KC)
                if k2 == KC - 1 and e2 >= ES - 1:
                    s.append(("gated", (b, e2)))
            if c % 2 == 1 and waiting:
                s.append(waiting.pop(0))
        assert not waiting
        s.append(("final", (b,)))
        s.append(("store", (b,)))
    return s


LAST_READER = {"xT": "dve", "projQ": "dve", "projK": "dve", "V": "dve", "score": "dve", "cols": "dve",
               "ctxT": "act", "ctxK": "act", "ctxV": "dve", "probT": "dve", "attn": "dve", "res1": "dve",
               "x1T": "act", "xq": "act", "xscore": "dve", "xpT": "act", "xout": "dve", "x2T": "act",
               "logit": "act", "xnT": "dve", "gatesT": "act", "gate_b": "act", "up": "dve", "final": "dve"}
PE_KINDS = list(LAST_READER) + ["outproj", "down"]
ACT_KINDS = ["xT", "split_wqkv", "projQ", "projK", "V", "score", "split_wout", "ctxT", "ctxK", "probT", "attn", "yT",
             "x1T", "xq", "xprob", "xpT", "x2T", "logit", "xnT", "gatesT", "gate_b", "gelu", "up"]
DVE_KINDS = ["xT", "split_wqkv", "projQ", "projK", "V", "score", "norm", "cols", "ctxV", "probT", "attn", "res1", "x1",
             "xscore", "xprob", "xout", "x2", "xr", "xnT", "gates", "up", "gated", "final", "store", "link", "mask",
             "bias", "split_ffn"]
POOL_KINDS = ["split_wout", "split_ffn", "res1", "xout", "x2", "gated", "final", "pool_link"]


def decoder_block(nc, a, out):
    SCHEDULE = build_schedule()
    ordinal, ring_of, ring, seen = {}, {}, [], {}
    for st in SCHEDULE:
        ordinal[st] = seen.get(st[0], 0)
        seen[st[0]] = ordinal[st] + 1
        if st[0] in LAST_READER:
            ring_of[st] = len(ring)
            ring.append(st)

    with ExitStack() as ctx:
        def sb(name, shape, dt=F32):
            return ctx.enter_context(nc.sbuf_tensor(name, shape, dt))

        rel = sb("rel", [P, N])
        ident = sb("ident", [P, P])
        earlier = sb("earlier", [P, ER * ER])
        pick = sb("pick", [32, ER * P], F32R)
        x_tok = sb("x_tok", [P, B * NT, C])
        xT_hi, xT_lo = sb("xT_hi", [P, B * N], F32R), sb("xT_lo", [P, B * N], F32R)
        stage = sb("stage", [P, 3 * HEADS * DH])
        pick_f = stage[0:32, 2 * HEADS * DH:3 * HEADS * DH]
        wq_hi, wq_lo = sb("wq_hi", [P, 3 * HEADS * DH], F32R), sb("wq_lo", [P, 3 * HEADS * DH], F32R)
        wo_hi, wo_lo = sb("wo_hi", [P, HEADS, C], F32R), sb("wo_lo", [P, HEADS, C], F32R)
        bias = sb("bias", [P, 4, N])
        q_hi, q_lo = sb("q_hi", [P, 2, N], F32R), sb("q_lo", [P, 2, N], F32R)
        k_hi, k_lo = sb("k_hi", [P, 2, N], F32R), sb("k_lo", [P, 2, N], F32R)
        v_hl = sb("v_hl", [P, NT, HEADS, 2 * DH], F32R)
        prob = sb("prob", [P, 2, 2 * HEAD_COLS])
        pT_hi, pT_lo = sb("pT_hi", [P, 2 * HEAD_COLS], F32R), sb("pT_lo", [P, 2 * HEAD_COLS], F32R)
        o_hi, o_lo = sb("o_hi", [P, 2, N], F32R), sb("o_lo", [P, 2, N], F32R)
        negmax, expsum, recip = sb("negmax", [P, 2, 8]), sb("expsum", [P, 2, 8]), sb("recip", [P, 2, 8])
        NROWS = E * KC + 5
        vec_rows, vec = sb("vec_rows", [NROWS, P]), sb("vec", [P, NROWS])
        B1, BOUT, BQ, BK, GS, GR = 0, E * KC, E * KC + 1, E * KC + 2, E * KC + 3, E * KC + 4
        wxq, wxk, wxv = sb("wxq", [P, C]), sb("wxk", [P, C]), sb("wxv", [P, C])
        ctx_tok, ctx_T = sb("ctx_tok", [S2, B, C]), sb("ctx_T", [P, B, S2])
        ctx_k, ctx_v = sb("ctx_k", [P, B, S2]), sb("ctx_v", [S2, B, C])
        bv_row = sb("bv_row", [S2, C])
        mask_i, keep, shut = sb("mask_i", [P, B, S2], I32), sb("keep", [P, B, S2]), sb("shut", [P, B, S2])
        yT_sb = sb("yT_sb", [P, N])
        xr_tok = yT_sb[:, :].rearrange("p (t c) -> p t c", t=NT)
        r_tok = sb("r_tok", [P, NT, C])
        x1_tok = sb("x1_tok", [P, NT, C])
        xT_sb = sb("xT_sb", [P, N])
        qx_sb = sb("qx_sb", [P, N])
        xs = sb("xs", [P, NT, S2])
        xsT = sb("xsT", [S2, N])
        small = sb("small", [P, 64])
        stats, mv = sb("stats", [P, NT, 6]), sb("mv", [P, NT, 2])
        x2_tok = sb("x2_tok", [P, B * NT, C])
        cent = sb("cent", [P, ER])
        b2 = sb("b2", [32, C])
        ez, sg = sb("ez", [P, NT, ER]), sb("sg", [P, NT, ER])
        cmp1, cmp2 = (qx_sb[:, i * 256:(i + 1) * 256].rearrange("p (a j) -> p a j", j=ER) for i in range(2))
        gates, gates_hl = sb("gates", [P, NT, ER]), sb("gates_hl", [P, NT, 32])
        g_hi = sb("g_hi", [P, NT, ER], F32R)
        gatesT = sb("gatesT", [32, B, N], F32R)
        gate_b = bias
        ffn_hi, ffn_lo = pT_hi, pT_lo
        acc = prob[:, 0, 0:B * N]
        part = prob[:, 1, 0:2 * N]
        out_tok = r_tok

        ring_bank = [ctx.enter_context(nc.psum_tensor(f"ring{i}", [P, 512], F32)) for i in range(BANKS)]
        sum_bank = [ctx.enter_context(nc.psum_tensor(f"sum{i}", [P, 512], F32)) for i in range(2)]

        def sem(name):
            return ctx.enter_context(nc.semaphore(name))

        filled = {k: sem(f"filled_{k}") for k in PE_KINDS}
        act_done = {k: sem(f"act_done_{k}") for k in ACT_KINDS}
        dve_done = {k: sem(f"dve_done_{k}") for k in DVE_KINDS}
        pool_done = {k: sem(f"pool_done_{k}") for k in POOL_KINDS}
        LOADS = ["consts", "x", "wq", "wk", "wv", "wout", "vecs", "xw", "ctx", "tail"]
        loaded = {k: sem(f"loaded_{k}") for k in LOADS}
        ffn_loaded = [sem(f"ffn_loaded_{i}") for i in range(FFN_SLOTS)]
        stored = sem("stored")
        block = ctx.enter_context(nc.Block())

        def bank(st):
            return ring_bank[ring_of[st] % BANKS]

        def released(st):
            done = {"act": act_done, "dve": dve_done}[LAST_READER[st[0]]]
            return done[st[0]], ordinal[st] + 1

        def ffn_w(w):
            at = (w % FFN_SLOTS) * 2 * HID
            return at, at + HID

        def xn(b, kind):
            if b == 0:
                return xT_hi[:, kind * N:(kind + 1) * N], xT_lo[:, kind * N:(kind + 1) * N]
            flat = v_hl[:, :, :, :].rearrange("p t h d -> p (t h d)")
            return (flat[:, 2 * kind * N:(2 * kind + 1) * N], flat[:, (2 * kind + 1) * N:(2 * kind + 2) * N])

        def y_index(b, e):
            return b * (ER + 1) + max(e - ES + 1, 0)

        @block.sync
        def _(sp):
            for t, n in ((rel, "rel"), (ident, "ident")):
                sp.dma_start(t[:, :], a[n]).then_inc(loaded["consts"], 16)
            x_v = a["x"].rearrange("b (t p) c -> p (b t) c", p=P)
            sp.dma_start(x_tok[:, :, :], x_v).then_inc(loaded["x"], 16)
            W = HEADS * DH
            for i, n in enumerate(("wq", "wk", "wv")):
                sp.dma_start(stage[:, i * W:(i + 1) * W],
                             a["L0_attn_w_qkv"][:, i * W:(i + 1) * W]).then_inc(loaded[n], 16)
            wo_v = a["L0_attn_w_out"].rearrange("(h d) c -> d h c", d=DH)
            wo_raw = prob[:, 1, 0:HEADS * C].rearrange("p (h c) -> p h c", h=HEADS)
            for half in range(2):
                sp.dma_start(wo_raw[half * DH:(half + 1) * DH, :, :], wo_v).then_inc(loaded["wout"], 16)
            at = 0
            for n, rows in (("L0_ffn_b1_s", ES * KC), ("L0_ffn_b1_r", ER * KC)):
                sp.dma_start(vec_rows[at:at + rows, :],
                             a[n].rearrange("e (k p) -> (e k) p", p=P)).then_inc(loaded["vecs"], 16)
                at += rows
            for n in ("L0_attn_b_out", "L0_xattn_bq", "L0_xattn_bk", "L0_ffn_g_shared", "L0_ffn_g_routed"):
                sp.dma_start(vec_rows[at:at + 1, :],
                             a[n].rearrange("(a c) -> a c", a=1)).then_inc(loaded["vecs"], 16)
                at += 1
            sp.dma_start(ctx_tok[:, :, :], a["ctx_1024"].rearrange("b s c -> s b c")).then_inc(loaded["ctx"], 16)
            for t, n in ((wxq, "Wq"), (wxk, "Wk"), (wxv, "Wv")):
                sp.dma_start(t[:, :], a["L0_xattn_" + n]).then_inc(loaded["xw"], 16)
            sp.dma_start(bv_row[:, :], a["L0_xattn_bv"].partition_broadcast(S2)).then_inc(loaded["xw"], 16)
            sp.dma_start(mask_i[:, :, :], a["mask_BxS2_if1"].partition_broadcast(P)).then_inc(loaded["tail"], 16)
            sp.dma_start(cent[:, :], a["L0_ffn_centroids"]).then_inc(loaded["tail"], 16)
            for at in (0, 16):
                if at:
                    sp.wait_ge(dve_done["link"], 1)
                else:
                    sp.wait_ge(dve_done["link"], 1)
                sp.dma_start(b2[at:at + ES, :], a["L0_ffn_b2_s"]).then_inc(loaded["tail"], 16)
                sp.dma_start(b2[at + ES:at + E, :], a["L0_ffn_b2_r"]).then_inc(loaded["tail"], 16)
            sp.dma_start(earlier[:, :], a["earlier"]).then_inc(loaded["tail"], 16)
            sp.wait_ge(dve_done["split_wqkv"], 6)
            sp.wait_ge(act_done["split_wqkv"], 6)
            sp.dma_start(pick_f, a["pick"]).then_inc(loaded["tail"], 16)
            for w in range(B * E):
                b, e = divmod(w, E)
                if w == FFN_SLOTS - 1:
                    sp.wait_ge(dve_done["mask"], 2)
                if w >= FFN_SLOTS:
                    sp.wait_ge(pool_done["split_ffn"], w - FFN_SLOTS + 1)
                s, i = ("s", e) if e < ES else ("r", e - ES)
                at = ffn_w(w)[0]
                sp.dma_start(stage[:, at:at + HID], a["L0_ffn_W1_" + s][i]).then_inc(ffn_loaded[w % FFN_SLOTS], 16)
                sp.dma_start(stage[:, at + HID:at + 2 * HID].rearrange("p (k c) -> p k c", k=KC),
                             a["L0_ffn_W2_" + s][i].rearrange("(k p) c -> p k c", p=P)).then_inc(ffn_loaded[w % FFN_SLOTS], 16)
                if w == E + 1 or w == B * E - 1:
                    bb = 0 if w == E + 1 else 1
                    sp.wait_ge(dve_done["store"], bb + 1)
                    sp.dma_start(out[bb].rearrange("(t p) c -> p t c", p=P), out_tok[:, :, :]).then_inc(stored, 16)
            sp.wait_ge(stored, 16 * B)

        @block.tensor
        def _(pe):

            def split3(dst, lhs_hi, lhs_lo, rhs_hi, rhs_lo, first=True, last=True):
                pe.matmul(dst, lhs_hi, rhs_hi, start=first, stop=False)
                pe.matmul(dst, lhs_lo, rhs_hi, start=False, stop=False)
                return pe.matmul(dst, lhs_hi, rhs_lo, start=False, stop=last)

            def turn(dst, src, p):
                return pe.transpose(dst, src, ident[0:p, 0:p])

            for st in SCHEDULE:
                kind, g = st
                if kind in LAST_READER:
                    n = ring_of[st]
                    if kind == "score" and g[2] == 1:
                        continue
                    upto = n + 1 if kind == "score" else n
                    for m in range(n, upto + 1):
                        if m >= BANKS:
                            done, count = released(ring[m - BANKS])
                            pe.wait_ge(done, count)
                    ps = bank(st)
                if kind == "xT":
                    b, = g
                    pe.wait_ge(loaded["consts"], 32)
                    pe.wait_ge(loaded["x"], 16)
                    for t in range(NT):
                        mm = turn(ps[:, t * P:(t + 1) * P], x_tok[:, b * NT + t, :], P)
                elif kind in ("projQ", "projK"):
                    u, = g
                    b, p = divmod(u, PAIRS)
                    i = kind == "projK"
                    pe.wait_ge(dve_done["xT"], b + 1)
                    pe.wait_ge(dve_done["split_wqkv"], 2 * i + p // 4 + 1)
                    at = i * HEADS * DH + p * P
                    mm = split3(ps[:, :], wq_hi[:, at:at + P], wq_lo[:, at:at + P],
                                xT_hi[:, b * N:(b + 1) * N], xT_lo[:, b * N:(b + 1) * N])
                elif kind == "V":
                    b, half, t = g
                    pe.wait_ge(dve_done["xT"], b + 1)
                    pe.wait_ge(dve_done["split_wqkv"], 5 + half)
                    at, tk = 2 * HEADS * DH + half * 512, b * N + t * P
                    mm = split3(ps[:, :], xT_hi[:, tk:tk + P], xT_lo[:, tk:tk + P],
                                wq_hi[:, at:at + 512], wq_lo[:, at:at + 512])
                elif kind == "score":
                    u, i, _ = g
                    pe.wait_ge(dve_done["projQ"], u + 1)
                    pe.wait_ge(dve_done["projK"], u + 1)
                    s, w = u % 2, P * (i + 1)
                    for n3, (l, r) in enumerate(((q_hi, k_hi), (q_lo, k_hi), (q_hi, k_lo))):
                        for j in range(2):
                            rows = slice(j * DH, (j + 1) * DH)
                            dst = ring_bank[(ring_of[st] + j) % BANKS]
                            mm = pe.matmul(dst[:, 0:w], l[rows, s, i * P:(i + 1) * P], r[rows, s, 0:w],
                                           start=n3 == 0, stop=n3 == 2)
                            if n3 == 2:
                                mm.then_inc(filled["score"], 1)
                    continue
                elif kind == "probT":
                    u, j, grp = g
                    pe.wait_ge(dve_done["norm"], NT * (u + 1))
                    for kt in GROUPS[grp]:
                        for i in range(kt, NT):
                            src = j * HEAD_COLS + ROW_AT[i] + kt * P
                            dst = KEY_AT[kt] - GROUP_AT[grp] + (i - kt) * P
                            mm = turn(ps[:, dst:dst + P], prob[:, u % 2, src:src + P], P)
                elif kind == "attn":
                    u, j = g
                    b, p = divmod(u, PAIRS)
                    h = 2 * p + j
                    pe.wait_ge(dve_done["probT"], 6 * u + 3 * j + 3)
                    pe.wait_ge(dve_done["V"], 8 * b + 4 * (h // 8) + 4)
                    for kt in range(NT):
                        w = N - kt * P
                        at = j * HEAD_COLS + KEY_AT[kt]
                        for n2, pt in enumerate((pT_hi, pT_lo)):
                            mm = pe.matmul(ps[:, kt * P:N], v_hl[:, kt, h, :], pt[:, at:at + w],
                                           start=kt == 0 and n2 == 0, stop=kt == NT - 1 and n2 == 1)
                elif kind == "outproj":
                    u, j = g
                    b, p = divmod(u, PAIRS)
                    h = 2 * p + j
                    pe.wait_ge(dve_done["attn"], 2 * u + j + 1)
                    pe.wait_ge(pool_done["split_wout"], 1)
                    mm = split3(sum_bank[b][:, :], wo_hi[:, h, :], wo_lo[:, h, :], o_hi[:, j, :], o_lo[:, j, :],
                                first=h == 0, last=h == HEADS - 1)
                elif kind == "cols":
                    pe.wait_ge(loaded["vecs"], 16 * 7)
                    mm = turn(ps[:, 0:NROWS], vec_rows[:, :], NROWS)
                elif kind == "ctxT":
                    pe.wait_ge(loaded["ctx"], 16)
                    for b in range(B):
                        mm = turn(ps[:, b * P:b * P + S2], ctx_tok[:, b, :], S2)
                elif kind == "ctxK":
                    pe.wait_ge(act_done["ctxT"], 1)
                    pe.wait_ge(loaded["xw"], 64)
                    mm = pe.matmul(ps[:, 0:B * S2], wxk[:, :], ctx_T[:, :, :].rearrange("p b s -> p (b s)"),
                                   start=True, stop=True)
                elif kind == "ctxV":
                    for b in range(B):
                        mm = pe.matmul(ps[0:S2, b * C:(b + 1) * C], ctx_T[:, b, :], wxv[:, :], start=True, stop=True)
                elif kind == "res1":
                    b, = g
                    pe.wait_ge(act_done["yT"], b + 1)
                    for t in range(NT):
                        mm = turn(ps[:, t * P:(t + 1) * P], yT_sb[:, t * P:(t + 1) * P], P)
                elif kind == "x1T":
                    b, = g
                    pe.wait_ge(dve_done["x1"], b + 1)
                    for t in range(NT):
                        mm = turn(ps[:, t * P:(t + 1) * P], x1_tok[:, t, :], P)
                elif kind == "xq":
                    b, = g
                    pe.wait_ge(act_done["x1T"], b + 1)
                    mm = pe.matmul(ps[:, :], wxq[:, :], xT_sb[:, :], start=True, stop=True)
                elif kind == "xscore":
                    b, = g
                    pe.wait_ge(act_done["xq"], b + 1)
                    pe.wait_ge(act_done["ctxK"], 2)
                    for t in range(NT):
                        mm = pe.matmul(ps[:, t * P:t * P + S2], qx_sb[:, t * P:(t + 1) * P], ctx_k[:, b, :],
                                       start=True, stop=True)
                elif kind == "xpT":
                    b, = g
                    pe.wait_ge(dve_done["xprob"], b + 1)
                    for t in range(NT):
                        mm = turn(ps[0:S2, t * P:(t + 1) * P], xs[:, t, :], P)
                elif kind == "xout":
                    b, = g
                    pe.wait_ge(act_done["xpT"], b + 1)
                    pe.wait_ge(dve_done["ctxV"], 1)
                    for t in range(NT):
                        mm = pe.matmul(ps[:, t * P:(t + 1) * P], xsT[:, t * P:(t + 1) * P], ctx_v[:, b, :],
                                       start=True, stop=True)
                elif kind == "x2T":
                    b, = g
                    pe.wait_ge(dve_done["x2"], 2 * b + 1)
                    for t in range(NT):
                        mm = turn(ps[:, t * P:(t + 1) * P], x2_tok[:, b * NT + t, :], P)
                elif kind == "logit":
                    b, = g
                    pe.wait_ge(act_done["x2T"], b + 1)
                    pe.wait_ge(loaded["tail"], 16 * 8)
                    for t in range(NT):
                        mm = pe.matmul(ps[:, t * ER:(t + 1) * ER], xT_sb[:, t * P:(t + 1) * P], cent[:, :],
                                       start=True, stop=True)
                elif kind == "xnT":
                    b, = g
                    pe.wait_ge(dve_done["xr"], b + 1)
                    for t in range(NT):
                        mm = turn(ps[:, t * P:(t + 1) * P], xr_tok[:, t, :], P)
                elif kind == "gatesT":
                    b, = g
                    pe.wait_ge(dve_done["gates"], b + 1)
                    for t in range(NT):
                        mm = turn(ps[0:32, t * P:(t + 1) * P], gates_hl[:, t, :], P)
                elif kind == "gate_b":
                    b, e = g
                    pe.wait_ge(act_done["gatesT"], b + 1)
                    pe.wait_ge(dve_done["mask"], 2)
                    mm = pe.matmul(ps[:, :], pick[:, (e - ES) * P:(e - ES + 1) * P], gatesT[:, b, :],
                                   start=True, stop=True)
                elif kind == "up":
                    b, c = g
                    e, k = divmod(c, KC)
                    pe.wait_ge(dve_done["xnT"], b + 1)
                    pe.wait_ge(pool_done["split_ffn"], b * E + e + 1)
                    x_hi, x_lo = xn(b, int(e >= ES))
                    at = ffn_w(b * E + e)[0] + k * P
                    mm = split3(ps[:, :], wq_hi[:, at:at + P], wq_lo[:, at:at + P], x_hi, x_lo)
                elif kind == "down":
                    b, c = g
                    e, k = divmod(c, KC)
                    m = y_index(b, e)
                    first = k == 0 and e in (0, *range(ES, E))
                    last = k == KC - 1 and e >= ES - 1
                    dst = sum_bank[m % 2][:, :]
                    if first and m < 2:
                        pe.wait_ge(act_done["yT"], m + 1)
                    elif first:
                        pe.wait_ge(dve_done["gated"], m - 1)
                    if first and e == 0:
                        pe.wait_ge(act_done["gatesT"], b + 1)
                        pe.wait_ge(loaded["tail"], 16 * 8)
                        pe.matmul(dst, b2[:, :], gatesT[:, b, :].bitcast(F32), start=True, stop=False)
                    pe.wait_ge(dve_done["up"], ordinal[("up", (b, c))] + 1)
                    at = ffn_w(b * E + e)[1] + k * P
                    gc = (c % 4) * 512
                    mm = split3(dst, wq_hi[:, at:at + P], wq_lo[:, at:at + P], ffn_hi[:, gc:gc + 512],
                                ffn_lo[:, gc:gc + 512], first=first and e != 0, last=last)
                elif kind == "final":
                    b, = g
                    pe.wait_ge(pool_done["gated"], (b + 1) * ER)
                    for t in range(NT):
                        mm = turn(ps[:, t * P:(t + 1) * P], acc[:, b * N + t * P:b * N + (t + 1) * P], P)
                else:
                    continue
                mm.then_inc(filled[kind], 1)

        @block.scalar
        def _(act):

            def copy(dst, src, scale=1.0):
                return act.activation(dst, src, ACT.Copy, scale=scale)

            def split_hi(n):
                act.wait_ge(loaded[("wq", "wk", "wv")[n // 2]], 16)
                copy(wq_hi[:, n * 512:(n + 1) * 512], stage[:, n * 512:(n + 1) * 512]).then_inc(act_done["split_wqkv"], 1)

            for st in SCHEDULE:
                kind, g = st
                if kind in LAST_READER and kind in ACT_KINDS and kind != "score":
                    act.wait_ge(filled[kind], ordinal[st] + 1)
                    ps = bank(st)
                if kind == "xT":
                    b, = g
                    op = copy(xT_hi[:, b * N:(b + 1) * N], ps[:, :])
                    op.then_inc(act_done["xT"], 1)
                    if b == 0:
                        for n in range(6):
                            split_hi(n)
                    continue
                elif kind in ("projQ", "projK"):
                    u, = g
                    if u >= 2:
                        act.wait_ge(filled["score"], 8 * (u - 1))
                    dst, scale = (q_hi, SCALE) if kind == "projQ" else (k_hi, 1.0)
                    op = copy(dst[:, u % 2, :], ps[:, :], scale)
                elif kind == "V":
                    b, half, t = g
                    if b == 1:
                        act.wait_ge(filled["attn"], 8 * (half + 1))
                    op = copy(v_hl[:, t, 8 * half:8 * half + 8, 0:DH], ps[:, :].rearrange("p (h d) -> p h d", d=DH))
                elif kind == "score":
                    u, i, j = g
                    s, w = u % 2, P * (i + 1)
                    at = j * HEAD_COLS + ROW_AT[i]
                    act.wait_ge(dve_done["score"], ordinal[st] + 1)
                    op = act.activation(prob[:, s, at:at + w], prob[:, s, at:at + w], ACT.Exp, scale=-1.0,
                                        bias=negmax[:, s, 2 * i + j:2 * i + j + 1],
                                        accum_out=expsum[:, s, 2 * i + j:2 * i + j + 1])
                elif kind == "split_wout":
                    act.wait_ge(loaded["wout"], 32)
                    op = copy(wo_hi[:, :, :].rearrange("p h c -> p (h c)"), prob[:, 1, 0:HEADS * C])
                elif kind == "probT":
                    u, j, grp = g
                    w = 256 if grp == 2 else 512
                    at = j * HEAD_COLS + GROUP_AT[grp]
                    if u >= 1:
                        act.wait_ge(filled["attn"], 2 * (u - 1) + j + 1)
                    op = copy(pT_hi[:, at:at + w], ps[:, 0:w])
                elif kind == "attn":
                    u, j = g
                    if u >= 1:
                        act.wait_ge(filled["outproj"], 2 * (u - 1) + j + 1)
                    op = copy(o_hi[:, j, :], ps[:, :])
                elif kind == "ctxT":
                    op = copy(ctx_T[:, :, :], ps[:, 0:B * P].rearrange("p (b s) -> p b s", b=B)[:, :, 0:S2])
                elif kind == "ctxK":
                    act.wait_ge(dve_done["cols"], 1)
                    act.activation(ctx_k[:, :, :], ps[:, 0:B * S2].rearrange("p (b s) -> p b s", b=B), ACT.Identity,
                                   bias=vec[:, BK:BK + 1]).then_inc(act_done["ctxK"], 2)
                    continue
                elif kind == "yT":
                    b, = g
                    act.wait_ge(filled["outproj"], HEADS * (b + 1))
                    act.wait_ge(dve_done["cols"], 1)
                    op = act.activation(yT_sb[:, :], sum_bank[b][:, :], ACT.Identity, bias=vec[:, BOUT:BOUT + 1])
                elif kind == "x1T":
                    op = copy(xT_sb[:, :], ps[:, :])
                elif kind == "xq":
                    op = act.activation(qx_sb[:, :], ps[:, :], ACT.Identity, bias=vec[:, BQ:BQ + 1])
                elif kind == "xprob":
                    b, = g
                    act.wait_ge(dve_done["xscore"], b + 1)
                    op = act.activation(xs[:, :, :], xs[:, :, :], ACT.Exp)
                elif kind == "xpT":
                    op = copy(xsT[:, :], ps[0:S2, :])
                elif kind == "x2T":
                    op = copy(xT_sb[:, :], ps[:, :])
                elif kind == "logit":
                    op = act.activation(ez[:, :, :].rearrange("p t e -> p (t e)"), ps[:, 0:NT * ER], ACT.Exp, scale=-1.0)
                elif kind == "xnT":
                    b, = g
                    if b == 0:
                        act.wait_ge(filled["projK"], UNITS)
                        act.wait_ge(filled["V"], 8 * B)
                    else:
                        act.wait_ge(filled["attn"], 2 * UNITS)
                    act.activation(xn(b, 0)[0], ps[:, :], ACT.Copy, scale=vec[:, GS:GS + 1])
                    op = act.activation(xn(b, 1)[0], ps[:, :], ACT.Copy, scale=vec[:, GR:GR + 1])
                elif kind == "gatesT":
                    b, = g
                    op = copy(gatesT[:, b, :], ps[0:32, :])
                elif kind == "gate_b":
                    b, e = g
                    m = b * ER + e - ES
                    if m >= 2:
                        pb, pe = divmod(m - 2, ER)
                        act.wait_ge(dve_done["gated"], y_index(pb, ES + pe) + 1)
                    else:
                        act.wait_ge(dve_done["score"], 8 * UNITS)
                    op = copy(gate_b[:, e % 2, :], ps[:, :])
                elif kind == "up":
                    b, c = g
                    e, k = divmod(c, KC)
                    o = ordinal[st]
                    gc = (c % 4) * 512
                    act.activation(ps[:, :], ps[:, :], ACT.Gelu, bias=vec[:, B1 + c:B1 + c + 1]).then_inc(act_done["gelu"], 1)
                    if o >= 4:
                        act.wait_ge(filled["down"], o - 3)
                    else:
                        act.wait_ge(filled["attn"], 2 * UNITS)
                    act.wait_ge(act_done["gelu"], o + 1)
                    op = copy(ffn_hi[:, gc:gc + 512], ps[:, :])
                else:
                    continue
                op.then_inc(act_done[kind], 1)

        @block.vector
        def _(dve):
            links = [1]

            def then(op):
                op.then_inc(dve_done["link"], 1)
                links[0] += 1
                dve.wait_ge(dve_done["link"], links[0])

            def token_stats(src):
                for t in range(NT):
                    last = dve.bn_stats(stats[:, t, :], src[:, t, :])
                then(last)
                for t in range(NT):
                    last = dve.bn_aggr(mv[:, t, :], stats[:, t, :])
                return last

            def normalise(dst, src, col):
                for t in range(NT):
                    last = dve.tensor_scalar(dst[:, t, :], src[:, t, :], mv[:, t, 0:1], small[:, col + t:col + t + 1],
                                             ALU.subtract, ALU.mult)
                return last

            def alibi(u):
                for j in range(2):
                    last = dve.tensor_scalar(bias[:, 2 * (u % 2) + j, :], rel[:, :], SLOPES[2 * (u % PAIRS) + j], None,
                                             ALU.mult)
                last.then_inc(dve_done["bias"], 1)

            dve.memset(b2[:, :], 0.0)
            dve.memset(gates_hl[:, :, :], 0.0).then_inc(dve_done["link"], 1)
            dve.wait_ge(loaded["consts"], 32)
            alibi(0)
            alibi(1)
            for st in SCHEDULE:
                kind, g = st
                if kind in LAST_READER and LAST_READER[kind] == "dve":
                    ps = bank(st)
                    if kind in ACT_KINDS and kind != "score":
                        dve.wait_ge(act_done[kind], ordinal[st] + 1)
                    else:
                        dve.wait_ge(filled[kind], ordinal[st] + 1)
                if kind == "xT":
                    b, = g
                    at = slice(b * N, (b + 1) * N)
                    dve.tensor_tensor(xT_lo[:, at], ps[:, :], xT_hi[:, at].bitcast(F32), ALU.subtract)\
                       .then_inc(dve_done["xT"], 1)
                    if b == 0:
                        for n in range(6):
                            at = slice(n * 512, (n + 1) * 512)
                            dve.wait_ge(act_done["split_wqkv"], n + 1)
                            dve.tensor_tensor(wq_lo[:, at], stage[:, at], wq_hi[:, at].bitcast(F32), ALU.subtract)\
                               .then_inc(dve_done["split_wqkv"], 1)
                    continue
                elif kind in ("projQ", "projK"):
                    u, = g
                    hi, lo, scale = (q_hi, q_lo, SCALE) if kind == "projQ" else (k_hi, k_lo, 1.0)
                    op = dve.scalar_tensor_tensor(lo[:, u % 2, :], ps[:, :], scale, hi[:, u % 2, :].bitcast(F32),
                                                  ALU.mult, ALU.subtract)
                elif kind == "V":
                    b, half, t = g
                    hs = slice(8 * half, 8 * half + 8)
                    op = dve.tensor_tensor(v_hl[:, t, hs, DH:2 * DH], ps[:, :].rearrange("p (h d) -> p h d", d=DH),
                                           v_hl[:, t, hs, 0:DH].bitcast(F32), ALU.subtract)
                elif kind == "score":
                    u, i, j = g
                    s, w = u % 2, P * (i + 1)
                    at = j * HEAD_COLS + ROW_AT[i]
                    dve.wait_ge(dve_done["bias"], u + 1)
                    if u >= 2:
                        dve.wait_ge(filled["probT"], 6 * (u - 1))
                    if u == 1:
                        dve.wait_ge(act_done["split_wout"], 1)
                        dve.wait_ge(pool_done["split_wout"], 1)
                    op = dve.tensor_tensor_reduce(out=prob[:, s, at:at + w], in0=ps[:, 0:w],
                                                  in1=bias[:, 2 * s + j, N - w:N], scale=-1.0, scalar=BIG,
                                                  op0=ALU.add, op1=ALU.min,
                                                  accum_out=negmax[:, s, 2 * i + j:2 * i + j + 1])
                elif kind == "norm":
                    u, i = g
                    s = u % 2
                    dve.wait_ge(act_done["score"], 8 * u + 2 * i + 2)
                    then(dve.reciprocal(recip[:, s, 2 * i:2 * i + 2], expsum[:, s, 2 * i:2 * i + 2]))
                    for j in range(2):
                        w = P * (i + 1)
                        at = j * HEAD_COLS + ROW_AT[i]
                        op = dve.tensor_scalar(prob[:, s, at:at + w], prob[:, s, at:at + w],
                                               recip[:, s, 2 * i + j:2 * i + j + 1], None, ALU.mult)
                    if i == NT - 1 and u + 2 < UNITS:
                        alibi(u + 2)
                elif kind == "split_ffn":
                    w, = g
                    both = slice(ffn_w(w)[0], ffn_w(w)[0] + 2 * HID)
                    dve.wait_ge(ffn_loaded[w % FFN_SLOTS], 32 * (w // FFN_SLOTS + 1))
                    if w < FFN_SLOTS:
                        dve.wait_ge(filled["projK"], UNITS)
                        dve.wait_ge(filled["V"], 8 * B)
                    else:
                        dve.wait_ge(filled["down"], KC * (w - FFN_SLOTS + 1))
                    op = dve.tensor_copy(wq_hi[:, both], stage[:, both])
                elif kind == "cols":
                    op = dve.tensor_copy(vec[:, :], ps[:, 0:NROWS])
                elif kind == "ctxV":
                    for b in range(B):
                        op = dve.tensor_tensor(ctx_v[:, b, :], ps[0:S2, b * C:(b + 1) * C], bv_row[:, :], ALU.add)
                    op.then_inc(dve_done["ctxV"], 1)
                    dve.wait_ge(loaded["tail"], 16 * 8)
                    dve.tensor_scalar(keep[:, :, :], mask_i[:, :, :], 0.0, None, ALU.not_equal)\
                       .then_inc(dve_done["mask"], 1)
                    dve.wait_ge(dve_done["mask"], 1)
                    dve.tensor_copy(pick[:, :], pick_f)
                    dve.tensor_scalar(shut[:, :, :], keep[:, :, :], 1.0, NEG, ALU.subtract, ALU.mult)\
                       .then_inc(dve_done["mask"], 1)
                    dve.wait_ge(dve_done["mask"], 2)
                    continue
                elif kind == "probT":
                    u, j, grp = g
                    w = 256 if grp == 2 else 512
                    at = j * HEAD_COLS + GROUP_AT[grp]
                    op = dve.tensor_tensor(pT_lo[:, at:at + w], ps[:, 0:w], pT_hi[:, at:at + w].bitcast(F32),
                                           ALU.subtract)
                elif kind == "attn":
                    u, j = g
                    op = dve.tensor_tensor(o_lo[:, j, :], ps[:, :], o_hi[:, j, :].bitcast(F32), ALU.subtract)
                elif kind == "res1":
                    b, = g
                    then(dve.tensor_tensor(r_tok[:, :, :], ps[:, :].rearrange("p (t c) -> p t c", t=NT),
                                           x_tok[:, b * NT:(b + 1) * NT, :], ALU.add))
                    op = token_stats(r_tok)
                elif kind == "x1":
                    b, = g
                    dve.wait_ge(pool_done["res1"], b + 1)
                    op = normalise(x1_tok, r_tok, 4)
                elif kind == "xscore":
                    b, = g
                    for t in range(NT):
                        last = dve.scalar_tensor_tensor(xs[:, t, :], ps[:, t * P:t * P + S2], XSCALE, keep[:, b, :],
                                                        ALU.mult, ALU.mult)
                    then(last)
                    then(dve.tensor_tensor(xs[:, :, :], xs[:, :, :],
                                           shut[:, b, :].unsqueeze(1).to_broadcast([P, NT, S2]), ALU.add))
                    then(dve.tensor_reduce(small[:, 8:12], xs[:, :, :], AXIS.X, ALU.max))
                    op = dve.tensor_tensor(xs[:, :, :], xs[:, :, :],
                                           small[:, 8:12].unsqueeze(2).to_broadcast([P, NT, S2]), ALU.subtract)
                elif kind == "xprob":
                    b, = g
                    dve.wait_ge(act_done["xprob"], b + 1)
                    then(dve.tensor_reduce(small[:, 12:16], xs[:, :, :], AXIS.X, ALU.add))
                    then(dve.reciprocal(small[:, 16:20], small[:, 12:16]))
                    op = dve.tensor_tensor(xs[:, :, :], xs[:, :, :],
                                           small[:, 16:20].unsqueeze(2).to_broadcast([P, NT, S2]), ALU.mult)
                elif kind == "xout":
                    b, = g
                    then(dve.tensor_tensor(r_tok[:, :, :], ps[:, :].rearrange("p (t c) -> p t c", t=NT),
                                           x1_tok[:, :, :], ALU.add))
                    op = token_stats(r_tok)
                elif kind == "x2":
                    b, = g
                    dve.wait_ge(pool_done["xout"], b + 1)
                    x2b = x2_tok[:, b * NT:(b + 1) * NT, :]
                    normalise(x2b, r_tok, 20).then_inc(dve_done["x2"], 1)
                    dve.wait_ge(dve_done["x2"], 2 * b + 1)
                    sq = qx_sb[:, :].rearrange("p (t c) -> p t c", t=NT)
                    then(dve.tensor_tensor(sq, x2b, x2b, ALU.mult))
                    op = dve.tensor_reduce(small[:, 24:28], sq, AXIS.X, ALU.add)
                elif kind == "xr":
                    b, = g
                    dve.wait_ge(pool_done["x2"], b + 1)
                    for t in range(NT):
                        op = dve.tensor_scalar(xr_tok[:, t, :], x2_tok[:, b * NT + t, :], small[:, 28 + t:29 + t], None,
                                               ALU.mult)
                elif kind == "xnT":
                    b, = g
                    for e in range(2):
                        hi, lo = xn(b, e)
                        op = dve.scalar_tensor_tensor(lo, ps[:, :], vec[:, GS + e:GS + e + 1], hi.bitcast(F32),
                                                      ALU.mult, ALU.subtract)
                elif kind == "gates":
                    b, = g
                    dve.wait_ge(act_done["logit"], b + 1)
                    flat = sg[:, :, :].rearrange("p t e -> p (t e)")
                    then(dve.tensor_scalar(gates[:, :, :], ez[:, :, :], 1.0, None, ALU.add))
                    then(dve.reciprocal(sg[:, :, :], gates[:, :, :]))
                    c1 = cmp1[:, :, :].rearrange("p (t e) j -> p t e j", t=NT)
                    c2 = cmp2[:, :, :].rearrange("p (t e) j -> p t e j", t=NT)
                    other = sg[:, :, :].unsqueeze(2).to_broadcast([P, NT, ER, ER])
                    own = sg[:, :, :].unsqueeze(3).to_broadcast([P, NT, ER, ER])
                    before = earlier[:, :].unsqueeze(1).to_broadcast([P, NT, ER * ER])
                    dve.tensor_tensor(c1, other, own, ALU.is_gt)
                    then(dve.tensor_tensor(c2, other, own, ALU.is_equal))
                    c2f = cmp2[:, :, :].rearrange("p (t e) j -> p t (e j)", t=NT)
                    then(dve.tensor_tensor(c2f, c2f, before, ALU.mult))
                    then(dve.tensor_tensor(cmp1[:, :, :], cmp1[:, :, :], cmp2[:, :, :], ALU.add))
                    then(dve.tensor_reduce(gates[:, :, :].rearrange("p t e -> p (t e)"), cmp1[:, :, :], AXIS.X, ALU.add))
                    then(dve.tensor_reduce(small[:, 32:36], sg[:, :, :], AXIS.X, ALU.add))
                    dve.reciprocal(small[:, 36:40], small[:, 32:36])
                    then(dve.tensor_scalar(gates[:, :, :], gates[:, :, :], 1.5, None, ALU.is_lt))
                    then(dve.tensor_tensor(gates[:, :, :], gates[:, :, :], sg[:, :, :], ALU.mult))
                    then(dve.tensor_tensor(gates[:, :, :], gates[:, :, :],
                                           small[:, 36:40].unsqueeze(2).to_broadcast([P, NT, ER]), ALU.mult))
                    then(dve.tensor_copy(g_hi[:, :, :], gates[:, :, :]))
                    dve.tensor_copy(gates_hl[:, :, ES:E], g_hi[:, :, :].bitcast(F32))
                    dve.memset(gates_hl[:, :, 0:ES], 1.0)
                    op = dve.tensor_tensor(gates_hl[:, :, 16 + ES:16 + E], gates[:, :, :], g_hi[:, :, :].bitcast(F32),
                                           ALU.subtract)
                elif kind == "up":
                    b, c = g
                    gc = (c % 4) * 512
                    op = dve.tensor_tensor(ffn_lo[:, gc:gc + 512], ps[:, :], ffn_hi[:, gc:gc + 512].bitcast(F32),
                                           ALU.subtract)
                elif kind == "gated":
                    b, e = g
                    m = y_index(b, e)
                    dve.wait_ge(filled["down"], ordinal[("down", (b, e * KC + KC - 1))] + 1)
                    if e < ES:
                        op = dve.tensor_copy(acc[:, b * N:(b + 1) * N], sum_bank[m % 2][:, :])
                    else:
                        i = b * ER + e - ES
                        dve.wait_ge(act_done["gate_b"], i + 1)
                        if i >= 2:
                            dve.wait_ge(pool_done["gated"], i - 1)
                        op = dve.tensor_tensor(part[:, (i % 2) * N:(i % 2 + 1) * N], sum_bank[m % 2][:, :],
                                               gate_b[:, e % 2, :], ALU.mult)
                elif kind == "final":
                    b, = g
                    if b == 1:
                        dve.wait_ge(stored, 16)
                    flat = x2_tok[:, b * NT:(b + 1) * NT, :].rearrange("p t c -> p (t c)")
                    then(dve.scalar_tensor_tensor(r_tok[:, :, :].rearrange("p t c -> p (t c)"), flat, 2.0, ps[:, :],
                                                  ALU.mult, ALU.add))
                    op = token_stats(r_tok)
                elif kind == "store":
                    b, = g
                    dve.wait_ge(pool_done["final"], b + 1)
                    op = normalise(out_tok, r_tok, 40)
                else:
                    continue
                op.then_inc(dve_done[kind], 1)

        @block.gpsimd
        def _(pool):
            links = [0]

            def then(op):
                op.then_inc(pool_done["pool_link"], 1)
                links[0] += 1
                pool.wait_ge(pool_done["pool_link"], links[0])

            def power(dst, src, scale, eps):
                then(pool.tensor_scalar(small[:, dst:dst + NT], src, scale, eps, ALU.mult, ALU.add))
                return pool.tensor_tensor(small[:, dst:dst + NT], small[:, dst:dst + NT], small[:, 0:NT], ALU.pow)

            then(pool.memset(small[:, 0:NT], -0.5))
            for st in SCHEDULE:
                kind, g = st
                if kind == "split_wout":
                    pool.wait_ge(act_done["split_wout"], 1)
                    pool.tensor_tensor(wo_lo[:, :, :].rearrange("p h c -> p (h c)"), prob[:, 1, 0:HEADS * C],
                                       wo_hi[:, :, :].rearrange("p h c -> p (h c)").bitcast(F32), ALU.subtract)\
                        .then_inc(pool_done["split_wout"], 1)
                elif kind == "split_ffn":
                    w, = g
                    both = slice(ffn_w(w)[0], ffn_w(w)[0] + 2 * HID)
                    pool.wait_ge(dve_done["split_ffn"], w + 1)
                    pool.tensor_tensor(wq_lo[:, both], stage[:, both], wq_hi[:, both].bitcast(F32), ALU.subtract)\
                        .then_inc(pool_done["split_ffn"], 1)
                elif kind == "res1":
                    b, = g
                    pool.wait_ge(dve_done["res1"], b + 1)
                    power(4, mv[:, :, 1], 1.0, LN_EPS).then_inc(pool_done["res1"], 1)
                elif kind == "xout":
                    b, = g
                    pool.wait_ge(dve_done["xout"], b + 1)
                    power(20, mv[:, :, 1], 1.0, LN_EPS).then_inc(pool_done["xout"], 1)
                elif kind == "x2":
                    b, = g
                    pool.wait_ge(dve_done["x2"], 2 * b + 2)
                    power(28, small[:, 24:28], 1.0 / C, RMS_EPS).then_inc(pool_done["x2"], 1)
                elif kind == "gated" and g[1] >= ES:
                    b, e = g
                    i = b * ER + e - ES
                    pool.wait_ge(dve_done["gated"], y_index(b, e) + 1)
                    if i:
                        pool.wait_ge(pool_done["gated"], i)
                    pool.tensor_tensor(acc[:, b * N:(b + 1) * N], acc[:, b * N:(b + 1) * N],
                                       part[:, (i % 2) * N:(i % 2 + 1) * N], ALU.add).then_inc(pool_done["gated"], 1)
                elif kind == "final":
                    b, = g
                    pool.wait_ge(dve_done["final"], b + 1)
                    power(40, mv[:, :, 1], 1.0, LN_EPS).then_inc(pool_done["final"], 1)


_INS = ['x', 'ctx_1024', 'mask_BxS2_if1', 'L0_attn_w_qkv', 'L0_attn_w_out', 'L0_attn_b_out', 'L0_xattn_Wq',
        'L0_xattn_bq', 'L0_xattn_Wk', 'L0_xattn_bk', 'L0_xattn_Wv', 'L0_xattn_bv', 'L0_ffn_g_shared', 'L0_ffn_W1_s',
        'L0_ffn_b1_s', 'L0_ffn_W2_s', 'L0_ffn_b2_s', 'L0_ffn_g_routed', 'L0_ffn_W1_r', 'L0_ffn_b1_r', 'L0_ffn_W2_r',
        'L0_ffn_b2_r', 'L0_ffn_centroids']


def shape_constants():
    import numpy as np
    p, c = np.arange(P)[:, None], np.arange(N)[None, :]
    rel = (c - p - (N - P)).astype(np.float32)
    rel = np.where(rel > 0, np.float32(-NEG * 100), rel).astype(np.float32)
    e = np.arange(ER)
    earlier = np.broadcast_to((e[None, :] < e[:, None]).astype(np.float32).reshape(1, -1), (P, ER * ER))
    pick = np.zeros((32, ER, P), np.float32)
    for k in range(ER):
        pick[ES + k, k] = pick[16 + ES + k, k] = 1.0
    return {"rel": rel, "ident": np.eye(P, dtype=np.float32), "earlier": np.ascontiguousarray(earlier),
            "pick": pick.reshape(32, ER * P)}


def kernel(**inputs):
    import numpy as np
    import concourse.bacc as bacc
    from concourse import mybir as mb
    from concourse.bass_utils import run_bass_kernel_spmd

    nc = bacc.Bacc("TRN2", target_bir_lowering=False, num_devices=1)
    arrays, aps = {}, {}
    for name, arr in [(n, inputs[n]) for n in _INS] + list(shape_constants().items()):
        arr = np.ascontiguousarray(arr)
        arrays[f"in_{name}"] = arr
        aps[name] = nc.dram_tensor(f"in_{name}", arr.shape, mb.dt.from_np(arr.dtype), kind="ExternalInput").ap()
    out = nc.dram_tensor("out_dram", (B, N, C), mb.dt.float32, kind="ExternalOutput").ap()
    decoder_block(nc, aps, out)
    r = run_bass_kernel_spmd(nc, [arrays], core_ids=[0])
    return r.results[0]["out_dram"]
```

```python
import concourse.bass as bass
from concourse import mybir
from contextlib import ExitStack

F32 = mybir.dt.float32
F32R = mybir.dt.float32r
I32 = mybir.dt.int32
ALU = mybir.AluOpType
ACT = mybir.ActivationFunctionType
AXIS = mybir.AxisListType

B, N, C = 2, 512, 128
HEADS, DH = 16, 64
S2 = 77
HID, ES, ER = 512, 2, 8
P = 128
NT = N // P
PAIRS = HEADS // 2
UNITS = B * PAIRS
KC = HID // P
E = ES + ER
CHUNKS = E * KC
SCALE = DH ** -0.5
XSCALE = float(C) ** -0.5
LN_EPS = 1e-5
RMS_EPS = 1.1920928955078125e-07
NEG = 1e30
BIG = 3e38
SLOPES = [(2.0 ** (-2.0 ** (-(4 - 3)))) ** (h + 1) for h in range(HEADS)]
BANKS = 6
ROW_AT = [sum(P * (k + 1) for k in range(i)) for i in range(NT)]
HEAD_COLS = ROW_AT[-1] + P * NT
GROUPS = [[0], [1, 3], [2]]
GROUP_AT = [0, 512, 1024]
KEY_AT = [0, 512, 1024, 896]
FFN_SLOTS = 3
FFN_BUFS = 5
LAG = 3


PE_ROUND = "S2 S1 S0 S3 TB1 TB2 TA0 K TA1 TA2 TB0 Q X3 YB X OA X2 OB YA".split()
ACT_ROUND = "S1 TB1 TB2 TA0 S0 K TA2 TA1 X3 TB0 S2 OA Q X OB X2 B S3".split()
DVE_ROUND = "S2 S1 N3 S0 S3 TB1 TB2 TA0 N0 K TA2 TA1 N1 X3 TB0 N2 OA Q X X2 OB".split()


def round_steps(token, u, extra):
    if token[0] == "X":
        return extra.get(token, [])
    i = "AB".find(token[1:2])
    kind, steps = {
        "S": (u, lambda v: [("score", (v, int(token[1]), j)) for j in range(2)]),
        "N": (u - (token == "N3"), lambda v: [("norm", (v, int(token[1])))]),
        "Q": (u + 1, lambda v: [("projQ", (v,))]),
        "K": (u + 1, lambda v: [("projK", (v,))]),
        "B": (u + 2, lambda v: [("alibi", (v,))]),
        "T": (u - 1, lambda v: [("probT", (v, i, int(token[2])))]),
        "O": (u - 1, lambda v: [("attn", (v, i))]),
        "Y": (u - 1 - i, lambda v: [("outproj", (v, i))]),
    }[token[0]]
    return steps(kind) if 0 <= kind < UNITS else []


def chain(b):
    return [(k, (b,)) for k in ("yT", "res1", "x1", "x1T", "xq", "xscore", "xprob", "xpT", "xout", "x2", "x2T", "xr",
                                "logit", "gates", "gatesT", "xnT")]


def build_schedules():
    head = [("xT", (0,)), ("projQ", (0,)), ("projK", (0,)), ("xT", (1,))]
    orders = {"pe": list(head), "act": list(head), "dve": list(head)}
    waiting = chain(0)
    for u in range(UNITS + 2):
        extra = {"X": [], "X2": [], "X3": []}
        first, second, third = [t for t in PE_ROUND if t in extra]
        if u == 0:
            extra[first] = [("cols", ()), ("split_wout", ())]
            extra[second] = [("V", (0, 0, t)) for t in range(NT)]
            extra[third] = [("V", (0, 1, t)) for t in range(NT)]
        elif u == 1:
            extra[first], extra[second], extra[third] = [("ctxT", ())], [("ctxK", ())], [("ctxV", ())]
        elif 5 <= u <= 8:
            extra["X"] = [("V", (1, 0, u - 5))]
        elif 9 <= u <= 12:
            extra["X"] = [("V", (1, 1, u - 9))]
        if 10 <= u <= 15:
            for x in (first, second, third):
                if waiting[0][0] != "xnT" and not extra[x]:
                    extra[x] = extra[x] + [waiting.pop(0)]
        if u in (15, 16):
            extra[third] = extra[third] + [("split_ffn", (n,)) for n in ((0, 1) if u == 15 else (2,))]
        if u == 16:
            extra[first] = waiting
        for order, tokens in (("pe", PE_ROUND), ("act", ACT_ROUND), ("dve", DVE_ROUND)):
            for token in tokens:
                orders[order] += round_steps(token, u, extra)
    ffn = []
    waiting = chain(1)
    for c in range(B * CHUNKS + LAG):
        b, cb = divmod(c, CHUNKS)
        e, k = divmod(cb, KC)
        if c < B * CHUNKS:
            if k == 1 and e >= ES:
                ffn.append(("gate_b", (b, e)))
            if k == KC - 1 and FFN_SLOTS <= b * E + e + 2 < B * E:
                ffn.append(("split_ffn", (b * E + e + 2,)))
            ffn.append(("up", (b, cb)))
        if c >= LAG:
            b2, cb2 = divmod(c - LAG, CHUNKS)
            e2, k2 = divmod(cb2, KC)
            ffn.append(("down", (b2, cb2)))
            if k2 == KC - 1 and e2 >= ES - 1:
                ffn.append(("gated", (b2, e2)))
        if c % 2 == 1 and waiting:
            ffn.append(waiting.pop(0))
        if c == CHUNKS + LAG + 5:
            ffn.append(("final", (0,)))
        if c == CHUNKS + LAG + 7:
            ffn.append(("store", (0,)))
    ffn += [("final", (1,)), ("store", (1,))]
    return [orders[k] + ffn for k in ("pe", "act", "dve")]


LAST_READER = {"xT": "dve", "projQ": "dve", "projK": "dve", "V": "dve", "score": "dve", "cols": "dve",
               "ctxT": "act", "ctxK": "act", "ctxV": "dve", "probT": "dve", "attn": "dve", "res1": "dve",
               "x1T": "act", "xq": "act", "xscore": "dve", "xpT": "act", "xout": "dve", "x2T": "act",
               "logit": "act", "xnT": "dve", "gatesT": "act", "gate_b": "act", "up": "dve", "final": "dve"}
PE_KINDS = list(LAST_READER) + ["outproj", "down"]
ACT_KINDS = ["xT", "split_wqkv", "projQ", "projK", "V", "score", "split_wout", "ctxT", "ctxK", "probT", "attn", "yT",
             "x1T", "xq", "xprob", "xpT", "x2T", "logit", "xnT", "gatesT", "gate_b", "gelu",
             "up", "alibi"]
DVE_KINDS = ["xT", "split_wqkv", "projQ", "projK", "V", "score", "norm", "cols", "ctxV", "probT", "attn", "res1", "x1",
             "xscore", "xprob", "xout", "x2", "xr", "xnT", "gates", "up", "gated", "final", "store", "link", "mask",
             "split_ffn"]
POOL_KINDS = ["split_wout", "split_ffn", "res1", "xout", "x2", "gated", "final", "pool_link"]


def decoder_block(nc, a, out):
    PE_STEPS, ACT_STEPS, DVE_STEPS = build_schedules()
    ring = [st for st in PE_STEPS if st[0] in LAST_READER]
    ring_of = {st: n for n, st in enumerate(ring)}

    def counts(steps):
        seen, out_ = {}, {}
        for st in steps:
            seen[st[0]] = seen.get(st[0], 0) + 1
            out_[st] = seen[st[0]]
        return out_

    pe_count, act_count, dve_count = counts(PE_STEPS), counts(ACT_STEPS), counts(DVE_STEPS)

    def all_of(count, kind, args):
        return max(count[(kind, g)] for g in args)

    with ExitStack() as ctx:
        def sb(name, shape, dt=F32):
            return ctx.enter_context(nc.sbuf_tensor(name, shape, dt))

        rel = sb("rel", [P, N])
        ident = sb("ident", [P, P])
        earlier = sb("earlier", [P, ER * ER])
        pick = sb("pick", [32, ER * P], F32R)
        x_tok = sb("x_tok", [P, B * NT, C])
        xT_hi, xT_lo = sb("xT_hi", [P, B * N], F32R), sb("xT_lo", [P, B * N], F32R)
        stage = sb("stage", [P, 3 * HEADS * DH])
        pick_f = stage[0:32, 2 * HEADS * DH:3 * HEADS * DH]
        wq_hi, wq_lo = sb("wq_hi", [P, 3 * HEADS * DH], F32R), sb("wq_lo", [P, 3 * HEADS * DH], F32R)
        wo_hi, wo_lo = sb("wo_hi", [P, HEADS, C], F32R), sb("wo_lo", [P, HEADS, C], F32R)
        bias = sb("bias", [P, 4, N])
        q_hi, q_lo = sb("q_hi", [P, 2, N], F32R), sb("q_lo", [P, 2, N], F32R)
        k_hi, k_lo = sb("k_hi", [P, 2, N], F32R), sb("k_lo", [P, 2, N], F32R)
        v_hl = sb("v_hl", [P, NT, HEADS, 2 * DH], F32R)
        prob = sb("prob", [P, 2, 2 * HEAD_COLS])
        pT_hi, pT_lo = sb("pT_hi", [P, 2 * HEAD_COLS], F32R), sb("pT_lo", [P, 2 * HEAD_COLS], F32R)
        o_hi, o_lo = sb("o_hi", [P, 2, N], F32R), sb("o_lo", [P, 2, N], F32R)
        negmax, expsum, recip = sb("negmax", [P, 2, 8]), sb("expsum", [P, 2, 8]), sb("recip", [P, 2, 8])
        NROWS = E * KC + 5
        vec_rows, vec = sb("vec_rows", [NROWS, P]), sb("vec", [P, NROWS])
        B1, BOUT, BQ, BK, GS, GR = 0, E * KC, E * KC + 1, E * KC + 2, E * KC + 3, E * KC + 4
        wxq, wxk, wxv = sb("wxq", [P, C]), sb("wxk", [P, C]), sb("wxv", [P, C])
        ctx_tok, ctx_T = sb("ctx_tok", [S2, B, C]), sb("ctx_T", [P, B, S2])
        ctx_k, ctx_v = sb("ctx_k", [P, B, S2]), sb("ctx_v", [S2, B, C])
        bv_row = sb("bv_row", [S2, C])
        mask_i, keep, shut = sb("mask_i", [P, B, S2], I32), sb("keep", [P, B, S2]), sb("shut", [P, B, S2])
        yT_sb = sb("yT_sb", [P, N])
        xr_tok = yT_sb[:, :].rearrange("p (t c) -> p t c", t=NT)
        r_tok = sb("r_tok", [P, NT, C])
        x1_tok = sb("x1_tok", [P, NT, C])
        xT_sb = sb("xT_sb", [P, N])
        qx_sb = sb("qx_sb", [P, N])
        xs = sb("xs", [P, NT, S2])
        xsT = sb("xsT", [S2, N])
        small = sb("small", [P, 64])
        stats, mv = sb("stats", [P, NT, 6]), sb("mv", [P, NT, 2])
        x2_tok = sb("x2_tok", [P, B * NT, C])
        cent = sb("cent", [P, ER])
        b2 = sb("b2", [32, C])
        ez, sg = sb("ez", [P, NT, ER]), sb("sg", [P, NT, ER])
        cmp1, cmp2 = (qx_sb[:, i * 256:(i + 1) * 256].rearrange("p (a j) -> p a j", j=ER) for i in range(2))
        gates, gates_hl = sb("gates", [P, NT, ER]), sb("gates_hl", [P, NT, 32])
        g_hi = sb("g_hi", [P, NT, ER], F32R)
        gatesT = sb("gatesT", [32, B, N], F32R)
        gate_b = bias
        ffn_hi, ffn_lo = pT_hi, pT_lo
        acc = prob[:, 0, 0:B * N]
        part = prob[:, 1, 0:2 * N]
        out_tok = r_tok

        ring_bank = [ctx.enter_context(nc.psum_tensor(f"ring{i}", [P, 512], F32)) for i in range(BANKS)]
        sum_bank = [ctx.enter_context(nc.psum_tensor(f"sum{i}", [P, 512], F32)) for i in range(2)]

        def sem(name):
            return ctx.enter_context(nc.semaphore(name))

        filled = {k: sem(f"filled_{k}") for k in PE_KINDS}
        act_done = {k: sem(f"act_done_{k}") for k in ACT_KINDS}
        dve_done = {k: sem(f"dve_done_{k}") for k in DVE_KINDS}
        pool_done = {k: sem(f"pool_done_{k}") for k in POOL_KINDS}
        LOADS = ["consts", "x", "wq", "wk", "wv", "wout", "vecs", "xw", "ctx", "tail"]
        loaded = {k: sem(f"loaded_{k}") for k in LOADS}
        ffn_loaded = [sem(f"ffn_loaded_{i}") for i in range(FFN_SLOTS)]
        stored = sem("stored")
        block = ctx.enter_context(nc.Block())

        def bank(st):
            return ring_bank[ring_of[st] % BANKS]

        def released(st):
            if LAST_READER[st[0]] == "act":
                return act_done[st[0]], act_count[st]
            return dve_done[st[0]], dve_count[st]

        def ffn_w(w):
            at = (w % FFN_SLOTS) * 2 * HID
            return at, at + HID

        def xn(b, kind):
            if b == 0:
                return xT_hi[:, kind * N:(kind + 1) * N], xT_lo[:, kind * N:(kind + 1) * N]
            flat = v_hl[:, :, :, :].rearrange("p t h d -> p (t h d)")
            return (flat[:, 2 * kind * N:(2 * kind + 1) * N], flat[:, (2 * kind + 1) * N:(2 * kind + 2) * N])

        def y_index(b, e):
            return b * (ER + 1) + max(e - ES + 1, 0)

        @block.sync
        def _(sp):
            for t, n in ((rel, "rel"), (ident, "ident")):
                sp.dma_start(t[:, :], a[n]).then_inc(loaded["consts"], 16)
            x_v = a["x"].rearrange("b (t p) c -> p (b t) c", p=P)
            sp.dma_start(x_tok[:, :, :], x_v).then_inc(loaded["x"], 16)
            W = HEADS * DH
            for i, n in enumerate(("wq", "wk", "wv")):
                sp.dma_start(stage[:, i * W:(i + 1) * W],
                             a["L0_attn_w_qkv"][:, i * W:(i + 1) * W]).then_inc(loaded[n], 16)
            wo_v = a["L0_attn_w_out"].rearrange("(h d) c -> d h c", d=DH)
            wo_raw = prob[:, 1, 0:HEADS * C].rearrange("p (h c) -> p h c", h=HEADS)
            for half in range(2):
                sp.dma_start(wo_raw[half * DH:(half + 1) * DH, :, :], wo_v).then_inc(loaded["wout"], 16)
            at = 0
            for n, rows in (("L0_ffn_b1_s", ES * KC), ("L0_ffn_b1_r", ER * KC)):
                sp.dma_start(vec_rows[at:at + rows, :],
                             a[n].rearrange("e (k p) -> (e k) p", p=P)).then_inc(loaded["vecs"], 16)
                at += rows
            for n in ("L0_attn_b_out", "L0_xattn_bq", "L0_xattn_bk", "L0_ffn_g_shared", "L0_ffn_g_routed"):
                sp.dma_start(vec_rows[at:at + 1, :],
                             a[n].rearrange("(a c) -> a c", a=1)).then_inc(loaded["vecs"], 16)
                at += 1
            sp.dma_start(ctx_tok[:, :, :], a["ctx_1024"].rearrange("b s c -> s b c")).then_inc(loaded["ctx"], 16)
            for t, n in ((wxq, "Wq"), (wxk, "Wk"), (wxv, "Wv")):
                sp.dma_start(t[:, :], a["L0_xattn_" + n]).then_inc(loaded["xw"], 16)
            sp.dma_start(bv_row[:, :], a["L0_xattn_bv"].partition_broadcast(S2)).then_inc(loaded["xw"], 16)
            sp.dma_start(mask_i[:, :, :], a["mask_BxS2_if1"].partition_broadcast(P)).then_inc(loaded["tail"], 16)
            sp.dma_start(cent[:, :], a["L0_ffn_centroids"]).then_inc(loaded["tail"], 16)
            for at in (0, 16):
                if at:
                    sp.wait_ge(dve_done["link"], 1)
                else:
                    sp.wait_ge(dve_done["link"], 1)
                sp.dma_start(b2[at:at + ES, :], a["L0_ffn_b2_s"]).then_inc(loaded["tail"], 16)
                sp.dma_start(b2[at + ES:at + E, :], a["L0_ffn_b2_r"]).then_inc(loaded["tail"], 16)
            sp.dma_start(earlier[:, :], a["earlier"]).then_inc(loaded["tail"], 16)
            sp.wait_ge(dve_done["split_wqkv"], 6)
            sp.wait_ge(act_done["split_wqkv"], 6)
            sp.dma_start(pick_f, a["pick"]).then_inc(loaded["tail"], 16)
            for w in range(B * E):
                b, e = divmod(w, E)
                if w == FFN_SLOTS - 1:
                    sp.wait_ge(dve_done["mask"], 2)
                if w >= FFN_SLOTS:
                    sp.wait_ge(pool_done["split_ffn"], w - FFN_SLOTS + 1)
                s, i = ("s", e) if e < ES else ("r", e - ES)
                at = ffn_w(w)[0]
                sp.dma_start(stage[:, at:at + HID], a["L0_ffn_W1_" + s][i]).then_inc(ffn_loaded[w % FFN_SLOTS], 16)
                sp.dma_start(stage[:, at + HID:at + 2 * HID].rearrange("p (k c) -> p k c", k=KC),
                             a["L0_ffn_W2_" + s][i].rearrange("(k p) c -> p k c", p=P)).then_inc(ffn_loaded[w % FFN_SLOTS], 16)
                if w == E + 3 or w == B * E - 1:
                    bb = int(w == B * E - 1)
                    sp.wait_ge(dve_done["store"], bb + 1)
                    sp.dma_start(out[bb].rearrange("(t p) c -> p t c", p=P), out_tok[:, :, :]).then_inc(stored, 16)
            sp.wait_ge(stored, 16 * B)

        @block.tensor
        def _(pe):

            def split3(dst, lhs_hi, lhs_lo, rhs_hi, rhs_lo, first=True, last=True):
                pe.matmul(dst, lhs_hi, rhs_hi, start=first, stop=False)
                pe.matmul(dst, lhs_lo, rhs_hi, start=False, stop=False)
                return pe.matmul(dst, lhs_hi, rhs_lo, start=False, stop=last)

            def turn(dst, src, p):
                return pe.transpose(dst, src, ident[0:p, 0:p])

            first_out = [min(pe_count[("outproj", (b * PAIRS + p, j))] for p in range(PAIRS) for j in range(2))
                         for b in range(B)]
            for st in PE_STEPS:
                kind, g = st
                if kind in LAST_READER:
                    n = ring_of[st]
                    if kind == "score" and g[2] == 1:
                        continue
                    upto = n + 1 if kind == "score" else n
                    for m in range(n, upto + 1):
                        if m >= BANKS:
                            done, count = released(ring[m - BANKS])
                            pe.wait_ge(done, count)
                    ps = bank(st)
                if kind == "xT":
                    b, = g
                    pe.wait_ge(loaded["consts"], 32)
                    pe.wait_ge(loaded["x"], 16)
                    for t in range(NT):
                        mm = turn(ps[:, t * P:(t + 1) * P], x_tok[:, b * NT + t, :], P)
                elif kind in ("projQ", "projK"):
                    u, = g
                    b, p = divmod(u, PAIRS)
                    i = kind == "projK"
                    pe.wait_ge(dve_done["xT"], b + 1)
                    pe.wait_ge(dve_done["split_wqkv"], 2 * i + p // 4 + 1)
                    at = i * HEADS * DH + p * P
                    mm = split3(ps[:, :], wq_hi[:, at:at + P], wq_lo[:, at:at + P],
                                xT_hi[:, b * N:(b + 1) * N], xT_lo[:, b * N:(b + 1) * N])
                elif kind == "V":
                    b, half, t = g
                    pe.wait_ge(dve_done["xT"], b + 1)
                    pe.wait_ge(dve_done["split_wqkv"], 5 + half)
                    at, tk = 2 * HEADS * DH + half * 512, b * N + t * P
                    mm = split3(ps[:, :], xT_hi[:, tk:tk + P], xT_lo[:, tk:tk + P],
                                wq_hi[:, at:at + 512], wq_lo[:, at:at + 512])
                elif kind == "score":
                    u, i, _ = g
                    pe.wait_ge(dve_done["projQ"], u + 1)
                    pe.wait_ge(dve_done["projK"], u + 1)
                    s, w = u % 2, P * (i + 1)
                    for n3, (l, r) in enumerate(((q_hi, k_hi), (q_lo, k_hi), (q_hi, k_lo))):
                        for j in range(2):
                            rows = slice(j * DH, (j + 1) * DH)
                            dst = ring_bank[(ring_of[st] + j) % BANKS]
                            mm = pe.matmul(dst[:, 0:w], l[rows, s, i * P:(i + 1) * P], r[rows, s, 0:w],
                                           start=n3 == 0, stop=n3 == 2)
                            if n3 == 2:
                                mm.then_inc(filled["score"], 1)
                    continue
                elif kind == "probT":
                    u, j, grp = g
                    pe.wait_ge(dve_done["norm"], all_of(dve_count, "norm", [(u, i) for i in range(NT)]))
                    for kt in GROUPS[grp]:
                        for i in range(kt, NT):
                            src = j * HEAD_COLS + ROW_AT[i] + kt * P
                            dst = KEY_AT[kt] - GROUP_AT[grp] + (i - kt) * P
                            mm = turn(ps[:, dst:dst + P], prob[:, u % 2, src:src + P], P)
                elif kind == "attn":
                    u, j = g
                    b, p = divmod(u, PAIRS)
                    h = 2 * p + j
                    pe.wait_ge(dve_done["probT"], all_of(dve_count, "probT", [(u, j, n) for n in range(3)]))
                    pe.wait_ge(dve_done["V"], 8 * b + 4 * (h // 8) + 4)
                    for kt in range(NT):
                        w = N - kt * P
                        at = j * HEAD_COLS + KEY_AT[kt]
                        for n2, pt in enumerate((pT_hi, pT_lo)):
                            mm = pe.matmul(ps[:, kt * P:N], v_hl[:, kt, h, :], pt[:, at:at + w],
                                           start=kt == 0 and n2 == 0, stop=kt == NT - 1 and n2 == 1)
                elif kind == "outproj":
                    u, j = g
                    b, p = divmod(u, PAIRS)
                    h = 2 * p + j
                    pe.wait_ge(dve_done["attn"], dve_count[("attn", (u, j))])
                    pe.wait_ge(pool_done["split_wout"], 1)
                    mm = split3(sum_bank[b][:, :], wo_hi[:, h, :], wo_lo[:, h, :], o_hi[:, j, :], o_lo[:, j, :],
                                first=pe_count[st] == first_out[b],
                                last=pe_count[st] == first_out[b] + HEADS - 1)
                elif kind == "cols":
                    pe.wait_ge(loaded["vecs"], 16 * 7)
                    mm = turn(ps[:, 0:NROWS], vec_rows[:, :], NROWS)
                elif kind == "ctxT":
                    pe.wait_ge(loaded["ctx"], 16)
                    for b in range(B):
                        mm = turn(ps[:, b * P:b * P + S2], ctx_tok[:, b, :], S2)
                elif kind == "ctxK":
                    pe.wait_ge(act_done["ctxT"], 1)
                    pe.wait_ge(loaded["xw"], 64)
                    mm = pe.matmul(ps[:, 0:B * S2], wxk[:, :], ctx_T[:, :, :].rearrange("p b s -> p (b s)"),
                                   start=True, stop=True)
                elif kind == "ctxV":
                    for b in range(B):
                        mm = pe.matmul(ps[0:S2, b * C:(b + 1) * C], ctx_T[:, b, :], wxv[:, :], start=True, stop=True)
                elif kind == "res1":
                    b, = g
                    pe.wait_ge(act_done["yT"], b + 1)
                    for t in range(NT):
                        mm = turn(ps[:, t * P:(t + 1) * P], yT_sb[:, t * P:(t + 1) * P], P)
                elif kind == "x1T":
                    b, = g
                    pe.wait_ge(dve_done["x1"], b + 1)
                    for t in range(NT):
                        mm = turn(ps[:, t * P:(t + 1) * P], x1_tok[:, t, :], P)
                elif kind == "xq":
                    b, = g
                    pe.wait_ge(act_done["x1T"], b + 1)
                    mm = pe.matmul(ps[:, :], wxq[:, :], xT_sb[:, :], start=True, stop=True)
                elif kind == "xscore":
                    b, = g
                    pe.wait_ge(act_done["xq"], b + 1)
                    pe.wait_ge(act_done["ctxK"], 1)
                    for t in range(NT):
                        mm = pe.matmul(ps[:, t * P:t * P + S2], qx_sb[:, t * P:(t + 1) * P], ctx_k[:, b, :],
                                       start=True, stop=True)
                elif kind == "xpT":
                    b, = g
                    pe.wait_ge(dve_done["xprob"], b + 1)
                    for t in range(NT):
                        mm = turn(ps[0:S2, t * P:(t + 1) * P], xs[:, t, :], P)
                elif kind == "xout":
                    b, = g
                    pe.wait_ge(act_done["xpT"], b + 1)
                    pe.wait_ge(dve_done["ctxV"], 1)
                    for t in range(NT):
                        mm = pe.matmul(ps[:, t * P:(t + 1) * P], xsT[:, t * P:(t + 1) * P], ctx_v[:, b, :],
                                       start=True, stop=True)
                elif kind == "x2T":
                    b, = g
                    pe.wait_ge(dve_done["x2"], 2 * b + 1)
                    for t in range(NT):
                        mm = turn(ps[:, t * P:(t + 1) * P], x2_tok[:, b * NT + t, :], P)
                elif kind == "logit":
                    b, = g
                    pe.wait_ge(act_done["x2T"], b + 1)
                    pe.wait_ge(loaded["tail"], 16 * 8)
                    for t in range(NT):
                        mm = pe.matmul(ps[:, t * ER:(t + 1) * ER], xT_sb[:, t * P:(t + 1) * P], cent[:, :],
                                       start=True, stop=True)
                elif kind == "xnT":
                    b, = g
                    pe.wait_ge(dve_done["xr"], b + 1)
                    for t in range(NT):
                        mm = turn(ps[:, t * P:(t + 1) * P], xr_tok[:, t, :], P)
                elif kind == "gatesT":
                    b, = g
                    pe.wait_ge(dve_done["gates"], b + 1)
                    for t in range(NT):
                        mm = turn(ps[0:32, t * P:(t + 1) * P], gates_hl[:, t, :], P)
                elif kind == "gate_b":
                    b, e = g
                    pe.wait_ge(act_done["gatesT"], b + 1)
                    pe.wait_ge(dve_done["mask"], 2)
                    mm = pe.matmul(ps[:, :], pick[:, (e - ES) * P:(e - ES + 1) * P], gatesT[:, b, :],
                                   start=True, stop=True)
                elif kind == "up":
                    b, c = g
                    e, k = divmod(c, KC)
                    pe.wait_ge(dve_done["xnT"], b + 1)
                    pe.wait_ge(pool_done["split_ffn"], b * E + e + 1)
                    x_hi, x_lo = xn(b, int(e >= ES))
                    at = ffn_w(b * E + e)[0] + k * P
                    mm = split3(ps[:, :], wq_hi[:, at:at + P], wq_lo[:, at:at + P], x_hi, x_lo)
                elif kind == "down":
                    b, c = g
                    e, k = divmod(c, KC)
                    m = y_index(b, e)
                    first = k == 0 and e in (0, *range(ES, E))
                    last = k == KC - 1 and e >= ES - 1
                    dst = sum_bank[m % 2][:, :]
                    if first and m < 2:
                        pe.wait_ge(act_done["yT"], m + 1)
                    elif first:
                        pe.wait_ge(dve_done["gated"], m - 1)
                    if first and e == 0:
                        pe.wait_ge(act_done["gatesT"], b + 1)
                        pe.wait_ge(loaded["tail"], 16 * 8)
                        pe.matmul(dst, b2[:, :], gatesT[:, b, :].bitcast(F32), start=True, stop=False)
                    pe.wait_ge(dve_done["up"], dve_count[("up", (b, c))])
                    at = ffn_w(b * E + e)[1] + k * P
                    gc = (dve_count[("up", (b, c))] - 1) % FFN_BUFS * 512
                    mm = split3(dst, wq_hi[:, at:at + P], wq_lo[:, at:at + P], ffn_hi[:, gc:gc + 512],
                                ffn_lo[:, gc:gc + 512], first=first and e != 0, last=last)
                elif kind == "final":
                    b, = g
                    pe.wait_ge(pool_done["gated"], (b + 1) * ER)
                    for t in range(NT):
                        mm = turn(ps[:, t * P:(t + 1) * P], acc[:, b * N + t * P:b * N + (t + 1) * P], P)
                else:
                    continue
                mm.then_inc(filled[kind], 1)

        @block.scalar
        def _(act):

            def copy(dst, src, scale=1.0):
                return act.activation(dst, src, ACT.Copy, scale=scale)

            def split_hi(n):
                act.wait_ge(loaded[("wq", "wk", "wv")[n // 2]], 16)
                copy(wq_hi[:, n * 512:(n + 1) * 512], stage[:, n * 512:(n + 1) * 512]).then_inc(act_done["split_wqkv"], 1)

            def alibi(u):
                for j in range(2):
                    last = copy(bias[:, 2 * (u % 2) + j, :], rel[:, :], SLOPES[2 * (u % PAIRS) + j])
                last.then_inc(act_done["alibi"], 1)

            act.wait_ge(loaded["consts"], 32)
            alibi(0)
            alibi(1)
            for st in ACT_STEPS:
                kind, g = st
                if kind in LAST_READER and kind in ACT_KINDS and kind != "score":
                    act.wait_ge(filled[kind], pe_count[st])
                    ps = bank(st)
                if kind == "xT":
                    b, = g
                    op = copy(xT_hi[:, b * N:(b + 1) * N], ps[:, :])
                    op.then_inc(act_done["xT"], 1)
                    if b == 0:
                        for n in range(6):
                            split_hi(n)
                    continue
                elif kind in ("projQ", "projK"):
                    u, = g
                    if u >= 2:
                        act.wait_ge(filled["score"], 8 * (u - 1))
                    dst, scale = (q_hi, SCALE) if kind == "projQ" else (k_hi, 1.0)
                    op = copy(dst[:, u % 2, :], ps[:, :], scale)
                elif kind == "V":
                    b, half, t = g
                    if b == 1:
                        act.wait_ge(filled["attn"], all_of(pe_count, "attn", [(4 * half + n, j) for n in range(4) for j in range(2)]))
                    op = copy(v_hl[:, t, 8 * half:8 * half + 8, 0:DH], ps[:, :].rearrange("p (h d) -> p h d", d=DH))
                elif kind == "score":
                    u, i, j = g
                    s, w = u % 2, P * (i + 1)
                    at = j * HEAD_COLS + ROW_AT[i]
                    act.wait_ge(dve_done["score"], dve_count[st])
                    op = act.activation(prob[:, s, at:at + w], prob[:, s, at:at + w], ACT.Exp, scale=-1.0,
                                        bias=negmax[:, s, 2 * i + j:2 * i + j + 1],
                                        accum_out=expsum[:, s, 2 * i + j:2 * i + j + 1])
                elif kind == "split_wout":
                    act.wait_ge(loaded["wout"], 32)
                    op = copy(wo_hi[:, :, :].rearrange("p h c -> p (h c)"), prob[:, 1, 0:HEADS * C])
                elif kind == "probT":
                    u, j, grp = g
                    w = 256 if grp == 2 else 512
                    at = j * HEAD_COLS + GROUP_AT[grp]
                    if u >= 1:
                        act.wait_ge(filled["attn"], pe_count[("attn", (u - 1, j))])
                    op = copy(pT_hi[:, at:at + w], ps[:, 0:w])
                elif kind == "attn":
                    u, j = g
                    if u >= 1:
                        act.wait_ge(filled["outproj"], pe_count[("outproj", (u - 1, j))])
                    op = copy(o_hi[:, j, :], ps[:, :])
                elif kind == "ctxT":
                    op = copy(ctx_T[:, :, :], ps[:, 0:B * P].rearrange("p (b s) -> p b s", b=B)[:, :, 0:S2])
                elif kind == "ctxK":
                    act.wait_ge(dve_done["cols"], 1)
                    op = act.activation(ctx_k[:, :, :], ps[:, 0:B * S2].rearrange("p (b s) -> p b s", b=B), ACT.Identity,
                                   bias=vec[:, BK:BK + 1])
                elif kind == "yT":
                    b, = g
                    act.wait_ge(filled["outproj"], all_of(pe_count, "outproj", [(b * PAIRS + p, j) for p in range(PAIRS) for j in range(2)]))
                    act.wait_ge(dve_done["cols"], 1)
                    op = act.activation(yT_sb[:, :], sum_bank[b][:, :], ACT.Identity, bias=vec[:, BOUT:BOUT + 1])
                elif kind == "x1T":
                    op = copy(xT_sb[:, :], ps[:, :])
                elif kind == "xq":
                    op = act.activation(qx_sb[:, :], ps[:, :], ACT.Identity, bias=vec[:, BQ:BQ + 1])
                elif kind == "xprob":
                    b, = g
                    act.wait_ge(dve_done["xscore"], b + 1)
                    op = act.activation(xs[:, :, :], xs[:, :, :], ACT.Exp)
                elif kind == "xpT":
                    op = copy(xsT[:, :], ps[0:S2, :])
                elif kind == "x2T":
                    op = copy(xT_sb[:, :], ps[:, :])
                elif kind == "logit":
                    op = act.activation(ez[:, :, :].rearrange("p t e -> p (t e)"), ps[:, 0:NT * ER], ACT.Exp, scale=-1.0)
                elif kind == "xnT":
                    b, = g
                    if b == 0:
                        act.wait_ge(filled["projK"], UNITS)
                        act.wait_ge(filled["V"], 8 * B)
                    else:
                        act.wait_ge(filled["attn"], 2 * UNITS)
                    act.activation(xn(b, 0)[0], ps[:, :], ACT.Copy, scale=vec[:, GS:GS + 1])
                    op = act.activation(xn(b, 1)[0], ps[:, :], ACT.Copy, scale=vec[:, GR:GR + 1])
                elif kind == "gatesT":
                    b, = g
                    op = copy(gatesT[:, b, :], ps[0:32, :])
                elif kind == "gate_b":
                    b, e = g
                    m = b * ER + e - ES
                    if m >= 2:
                        pb, pe = divmod(m - 2, ER)
                        act.wait_ge(dve_done["gated"], y_index(pb, ES + pe) + 1)
                    else:
                        act.wait_ge(dve_done["score"], 8 * UNITS)
                    op = copy(gate_b[:, e % 2, :], ps[:, :])
                elif kind == "up":
                    b, c = g
                    e, k = divmod(c, KC)
                    o = act_count[st] - 1
                    gc = o % FFN_BUFS * 512
                    act.activation(ps[:, :], ps[:, :], ACT.Gelu, bias=vec[:, B1 + c:B1 + c + 1]).then_inc(act_done["gelu"], 1)
                    if o >= FFN_BUFS:
                        act.wait_ge(filled["down"], o - FFN_BUFS + 1)
                    else:
                        act.wait_ge(filled["attn"], 2 * UNITS)
                    act.wait_ge(act_done["gelu"], o + 1)
                    op = copy(ffn_hi[:, gc:gc + 512], ps[:, :])
                elif kind == "alibi":
                    u, = g
                    act.wait_ge(dve_done["score"], all_of(dve_count, "score", [(u - 2, i, j) for i in range(NT) for j in range(2)]))
                    alibi(u)
                    continue
                else:
                    continue
                op.then_inc(act_done[kind], 1)

        @block.vector
        def _(dve):
            links = [1]

            def then(op):
                op.then_inc(dve_done["link"], 1)
                links[0] += 1
                dve.wait_ge(dve_done["link"], links[0])

            def token_stats(src):
                for t in range(NT):
                    last = dve.bn_stats(stats[:, t, :], src[:, t, :])
                then(last)
                for t in range(NT):
                    last = dve.bn_aggr(mv[:, t, :], stats[:, t, :])
                return last

            def normalise(dst, src, col):
                for t in range(NT):
                    last = dve.tensor_scalar(dst[:, t, :], src[:, t, :], mv[:, t, 0:1], small[:, col + t:col + t + 1],
                                             ALU.subtract, ALU.mult)
                return last

            dve.memset(b2[:, :], 0.0)
            dve.memset(gates_hl[:, :, :], 0.0).then_inc(dve_done["link"], 1)
            for st in DVE_STEPS:
                kind, g = st
                if kind in LAST_READER and LAST_READER[kind] == "dve":
                    ps = bank(st)
                    if kind in ACT_KINDS and kind != "score":
                        dve.wait_ge(act_done[kind], act_count[st])
                    else:
                        dve.wait_ge(filled[kind], pe_count[st])
                if kind == "xT":
                    b, = g
                    at = slice(b * N, (b + 1) * N)
                    dve.tensor_tensor(xT_lo[:, at], ps[:, :], xT_hi[:, at].bitcast(F32), ALU.subtract)\
                       .then_inc(dve_done["xT"], 1)
                    if b == 0:
                        for n in range(6):
                            at = slice(n * 512, (n + 1) * 512)
                            dve.wait_ge(act_done["split_wqkv"], n + 1)
                            dve.tensor_tensor(wq_lo[:, at], stage[:, at], wq_hi[:, at].bitcast(F32), ALU.subtract)\
                               .then_inc(dve_done["split_wqkv"], 1)
                    continue
                elif kind in ("projQ", "projK"):
                    u, = g
                    hi, lo, scale = (q_hi, q_lo, SCALE) if kind == "projQ" else (k_hi, k_lo, 1.0)
                    op = dve.scalar_tensor_tensor(lo[:, u % 2, :], ps[:, :], scale, hi[:, u % 2, :].bitcast(F32),
                                                  ALU.mult, ALU.subtract)
                elif kind == "V":
                    b, half, t = g
                    hs = slice(8 * half, 8 * half + 8)
                    op = dve.tensor_tensor(v_hl[:, t, hs, DH:2 * DH], ps[:, :].rearrange("p (h d) -> p h d", d=DH),
                                           v_hl[:, t, hs, 0:DH].bitcast(F32), ALU.subtract)
                elif kind == "score":
                    u, i, j = g
                    s, w = u % 2, P * (i + 1)
                    at = j * HEAD_COLS + ROW_AT[i]
                    dve.wait_ge(act_done["alibi"], u + 1)
                    if u >= 2:
                        dve.wait_ge(filled["probT"], 6 * (u - 1))
                    if u == 1:
                        dve.wait_ge(act_done["split_wout"], 1)
                        dve.wait_ge(pool_done["split_wout"], 1)
                    op = dve.tensor_tensor_reduce(out=prob[:, s, at:at + w], in0=ps[:, 0:w],
                                                  in1=bias[:, 2 * s + j, N - w:N], scale=-1.0, scalar=BIG,
                                                  op0=ALU.add, op1=ALU.min,
                                                  accum_out=negmax[:, s, 2 * i + j:2 * i + j + 1])
                elif kind == "norm":
                    u, i = g
                    s = u % 2
                    dve.wait_ge(act_done["score"], all_of(act_count, "score", [(u, i, j) for j in range(2)]))
                    then(dve.reciprocal(recip[:, s, 2 * i:2 * i + 2], expsum[:, s, 2 * i:2 * i + 2]))
                    for j in range(2):
                        w = P * (i + 1)
                        at = j * HEAD_COLS + ROW_AT[i]
                        op = dve.tensor_scalar(prob[:, s, at:at + w], prob[:, s, at:at + w],
                                               recip[:, s, 2 * i + j:2 * i + j + 1], None, ALU.mult)
                elif kind == "split_ffn":
                    w, = g
                    both = slice(ffn_w(w)[0], ffn_w(w)[0] + 2 * HID)
                    dve.wait_ge(ffn_loaded[w % FFN_SLOTS], 32 * (w // FFN_SLOTS + 1))
                    if w < FFN_SLOTS:
                        dve.wait_ge(filled["projK"], UNITS)
                        dve.wait_ge(filled["V"], 8 * B)
                    else:
                        dve.wait_ge(filled["down"], KC * (w - FFN_SLOTS + 1))
                    op = dve.tensor_copy(wq_hi[:, both], stage[:, both])
                elif kind == "cols":
                    op = dve.tensor_copy(vec[:, :], ps[:, 0:NROWS])
                elif kind == "ctxV":
                    for b in range(B):
                        op = dve.tensor_tensor(ctx_v[:, b, :], ps[0:S2, b * C:(b + 1) * C], bv_row[:, :], ALU.add)
                    op.then_inc(dve_done["ctxV"], 1)
                    dve.wait_ge(loaded["tail"], 16 * 8)
                    dve.tensor_scalar(keep[:, :, :], mask_i[:, :, :], 0.0, None, ALU.not_equal)\
                       .then_inc(dve_done["mask"], 1)
                    dve.wait_ge(dve_done["mask"], 1)
                    dve.tensor_copy(pick[:, :], pick_f)
                    dve.tensor_scalar(shut[:, :, :], keep[:, :, :], 1.0, NEG, ALU.subtract, ALU.mult)\
                       .then_inc(dve_done["mask"], 1)
                    dve.wait_ge(dve_done["mask"], 2)
                    continue
                elif kind == "probT":
                    u, j, grp = g
                    w = 256 if grp == 2 else 512
                    at = j * HEAD_COLS + GROUP_AT[grp]
                    op = dve.tensor_tensor(pT_lo[:, at:at + w], ps[:, 0:w], pT_hi[:, at:at + w].bitcast(F32),
                                           ALU.subtract)
                elif kind == "attn":
                    u, j = g
                    op = dve.tensor_tensor(o_lo[:, j, :], ps[:, :], o_hi[:, j, :].bitcast(F32), ALU.subtract)
                elif kind == "res1":
                    b, = g
                    then(dve.tensor_tensor(r_tok[:, :, :], ps[:, :].rearrange("p (t c) -> p t c", t=NT),
                                           x_tok[:, b * NT:(b + 1) * NT, :], ALU.add))
                    op = token_stats(r_tok)
                elif kind == "x1":
                    b, = g
                    dve.wait_ge(pool_done["res1"], b + 1)
                    op = normalise(x1_tok, r_tok, 4)
                elif kind == "xscore":
                    b, = g
                    for t in range(NT):
                        last = dve.scalar_tensor_tensor(xs[:, t, :], ps[:, t * P:t * P + S2], XSCALE, keep[:, b, :],
                                                        ALU.mult, ALU.mult)
                    then(last)
                    then(dve.tensor_tensor(xs[:, :, :], xs[:, :, :],
                                           shut[:, b, :].unsqueeze(1).to_broadcast([P, NT, S2]), ALU.add))
                    then(dve.tensor_reduce(small[:, 8:12], xs[:, :, :], AXIS.X, ALU.max))
                    op = dve.tensor_tensor(xs[:, :, :], xs[:, :, :],
                                           small[:, 8:12].unsqueeze(2).to_broadcast([P, NT, S2]), ALU.subtract)
                elif kind == "xprob":
                    b, = g
                    dve.wait_ge(act_done["xprob"], b + 1)
                    then(dve.tensor_reduce(small[:, 12:16], xs[:, :, :], AXIS.X, ALU.add))
                    then(dve.reciprocal(small[:, 16:20], small[:, 12:16]))
                    op = dve.tensor_tensor(xs[:, :, :], xs[:, :, :],
                                           small[:, 16:20].unsqueeze(2).to_broadcast([P, NT, S2]), ALU.mult)
                elif kind == "xout":
                    b, = g
                    then(dve.tensor_tensor(r_tok[:, :, :], ps[:, :].rearrange("p (t c) -> p t c", t=NT),
                                           x1_tok[:, :, :], ALU.add))
                    op = token_stats(r_tok)
                elif kind == "x2":
                    b, = g
                    dve.wait_ge(pool_done["xout"], b + 1)
                    x2b = x2_tok[:, b * NT:(b + 1) * NT, :]
                    normalise(x2b, r_tok, 20).then_inc(dve_done["x2"], 1)
                    dve.wait_ge(dve_done["x2"], 2 * b + 1)
                    sq = qx_sb[:, :].rearrange("p (t c) -> p t c", t=NT)
                    then(dve.tensor_tensor(sq, x2b, x2b, ALU.mult))
                    op = dve.tensor_reduce(small[:, 24:28], sq, AXIS.X, ALU.add)
                elif kind == "xr":
                    b, = g
                    dve.wait_ge(pool_done["x2"], b + 1)
                    for t in range(NT):
                        op = dve.tensor_scalar(xr_tok[:, t, :], x2_tok[:, b * NT + t, :], small[:, 28 + t:29 + t], None,
                                               ALU.mult)
                elif kind == "xnT":
                    b, = g
                    for e in range(2):
                        hi, lo = xn(b, e)
                        op = dve.scalar_tensor_tensor(lo, ps[:, :], vec[:, GS + e:GS + e + 1], hi.bitcast(F32),
                                                      ALU.mult, ALU.subtract)
                elif kind == "gates":
                    b, = g
                    dve.wait_ge(act_done["logit"], b + 1)
                    flat = sg[:, :, :].rearrange("p t e -> p (t e)")
                    then(dve.tensor_scalar(gates[:, :, :], ez[:, :, :], 1.0, None, ALU.add))
                    then(dve.reciprocal(sg[:, :, :], gates[:, :, :]))
                    c1 = cmp1[:, :, :].rearrange("p (t e) j -> p t e j", t=NT)
                    c2 = cmp2[:, :, :].rearrange("p (t e) j -> p t e j", t=NT)
                    other = sg[:, :, :].unsqueeze(2).to_broadcast([P, NT, ER, ER])
                    own = sg[:, :, :].unsqueeze(3).to_broadcast([P, NT, ER, ER])
                    before = earlier[:, :].unsqueeze(1).to_broadcast([P, NT, ER * ER])
                    dve.tensor_tensor(c1, other, own, ALU.is_gt)
                    then(dve.tensor_tensor(c2, other, own, ALU.is_equal))
                    c2f = cmp2[:, :, :].rearrange("p (t e) j -> p t (e j)", t=NT)
                    then(dve.tensor_tensor(c2f, c2f, before, ALU.mult))
                    then(dve.tensor_tensor(cmp1[:, :, :], cmp1[:, :, :], cmp2[:, :, :], ALU.add))
                    then(dve.tensor_reduce(gates[:, :, :].rearrange("p t e -> p (t e)"), cmp1[:, :, :], AXIS.X, ALU.add))
                    then(dve.tensor_reduce(small[:, 32:36], sg[:, :, :], AXIS.X, ALU.add))
                    dve.reciprocal(small[:, 36:40], small[:, 32:36])
                    then(dve.tensor_scalar(gates[:, :, :], gates[:, :, :], 1.5, None, ALU.is_lt))
                    then(dve.tensor_tensor(gates[:, :, :], gates[:, :, :], sg[:, :, :], ALU.mult))
                    then(dve.tensor_tensor(gates[:, :, :], gates[:, :, :],
                                           small[:, 36:40].unsqueeze(2).to_broadcast([P, NT, ER]), ALU.mult))
                    then(dve.tensor_copy(g_hi[:, :, :], gates[:, :, :]))
                    dve.tensor_copy(gates_hl[:, :, ES:E], g_hi[:, :, :].bitcast(F32))
                    dve.memset(gates_hl[:, :, 0:ES], 1.0)
                    op = dve.tensor_tensor(gates_hl[:, :, 16 + ES:16 + E], gates[:, :, :], g_hi[:, :, :].bitcast(F32),
                                           ALU.subtract)
                elif kind == "up":
                    b, c = g
                    gc = (dve_count[st] - 1) % FFN_BUFS * 512
                    op = dve.tensor_tensor(ffn_lo[:, gc:gc + 512], ps[:, :], ffn_hi[:, gc:gc + 512].bitcast(F32),
                                           ALU.subtract)
                elif kind == "gated":
                    b, e = g
                    m = y_index(b, e)
                    dve.wait_ge(filled["down"], pe_count[("down", (b, e * KC + KC - 1))])
                    if e < ES:
                        op = dve.tensor_copy(acc[:, b * N:(b + 1) * N], sum_bank[m % 2][:, :])
                    else:
                        i = b * ER + e - ES
                        dve.wait_ge(act_done["gate_b"], i + 1)
                        if i >= 2:
                            dve.wait_ge(pool_done["gated"], i - 1)
                        op = dve.tensor_tensor(part[:, (i % 2) * N:(i % 2 + 1) * N], sum_bank[m % 2][:, :],
                                               gate_b[:, e % 2, :], ALU.mult)
                elif kind == "final":
                    b, = g
                    if b == 1:
                        dve.wait_ge(stored, 16)
                    flat = x2_tok[:, b * NT:(b + 1) * NT, :].rearrange("p t c -> p (t c)")
                    then(dve.scalar_tensor_tensor(r_tok[:, :, :].rearrange("p t c -> p (t c)"), flat, 2.0, ps[:, :],
                                                  ALU.mult, ALU.add))
                    op = token_stats(r_tok)
                elif kind == "store":
                    b, = g
                    dve.wait_ge(pool_done["final"], b + 1)
                    op = normalise(out_tok, r_tok, 40)
                else:
                    continue
                op.then_inc(dve_done[kind], 1)

        @block.gpsimd
        def _(pool):
            links = [0]

            def then(op):
                op.then_inc(pool_done["pool_link"], 1)
                links[0] += 1
                pool.wait_ge(pool_done["pool_link"], links[0])

            def power(dst, src, scale, eps):
                then(pool.tensor_scalar(small[:, dst:dst + NT], src, scale, eps, ALU.mult, ALU.add))
                return pool.tensor_tensor(small[:, dst:dst + NT], small[:, dst:dst + NT], small[:, 0:NT], ALU.pow)

            then(pool.memset(small[:, 0:NT], -0.5))
            for st in DVE_STEPS:
                kind, g = st
                if kind == "split_wout":
                    pool.wait_ge(act_done["split_wout"], 1)
                    pool.tensor_tensor(wo_lo[:, :, :].rearrange("p h c -> p (h c)"), prob[:, 1, 0:HEADS * C],
                                       wo_hi[:, :, :].rearrange("p h c -> p (h c)").bitcast(F32), ALU.subtract)\
                        .then_inc(pool_done["split_wout"], 1)
                elif kind == "split_ffn":
                    w, = g
                    both = slice(ffn_w(w)[0], ffn_w(w)[0] + 2 * HID)
                    pool.wait_ge(dve_done["split_ffn"], w + 1)
                    pool.tensor_tensor(wq_lo[:, both], stage[:, both], wq_hi[:, both].bitcast(F32), ALU.subtract)\
                        .then_inc(pool_done["split_ffn"], 1)
                elif kind == "res1":
                    b, = g
                    pool.wait_ge(dve_done["res1"], b + 1)
                    power(4, mv[:, :, 1], 1.0, LN_EPS).then_inc(pool_done["res1"], 1)
                elif kind == "xout":
                    b, = g
                    pool.wait_ge(dve_done["xout"], b + 1)
                    power(20, mv[:, :, 1], 1.0, LN_EPS).then_inc(pool_done["xout"], 1)
                elif kind == "x2":
                    b, = g
                    pool.wait_ge(dve_done["x2"], 2 * b + 2)
                    power(28, small[:, 24:28], 1.0 / C, RMS_EPS).then_inc(pool_done["x2"], 1)
                elif kind == "gated" and g[1] >= ES:
                    b, e = g
                    i = b * ER + e - ES
                    pool.wait_ge(dve_done["gated"], y_index(b, e) + 1)
                    if i:
                        pool.wait_ge(pool_done["gated"], i)
                    pool.tensor_tensor(acc[:, b * N:(b + 1) * N], acc[:, b * N:(b + 1) * N],
                                       part[:, (i % 2) * N:(i % 2 + 1) * N], ALU.add).then_inc(pool_done["gated"], 1)
                elif kind == "final":
                    b, = g
                    pool.wait_ge(dve_done["final"], b + 1)
                    power(40, mv[:, :, 1], 1.0, LN_EPS).then_inc(pool_done["final"], 1)


_INS = ['x', 'ctx_1024', 'mask_BxS2_if1', 'L0_attn_w_qkv', 'L0_attn_w_out', 'L0_attn_b_out', 'L0_xattn_Wq',
        'L0_xattn_bq', 'L0_xattn_Wk', 'L0_xattn_bk', 'L0_xattn_Wv', 'L0_xattn_bv', 'L0_ffn_g_shared', 'L0_ffn_W1_s',
        'L0_ffn_b1_s', 'L0_ffn_W2_s', 'L0_ffn_b2_s', 'L0_ffn_g_routed', 'L0_ffn_W1_r', 'L0_ffn_b1_r', 'L0_ffn_W2_r',
        'L0_ffn_b2_r', 'L0_ffn_centroids']


def shape_constants():
    import numpy as np
    p, c = np.arange(P)[:, None], np.arange(N)[None, :]
    rel = (c - p - (N - P)).astype(np.float32)
    rel = np.where(rel > 0, np.float32(-NEG * 100), rel).astype(np.float32)
    e = np.arange(ER)
    earlier = np.broadcast_to((e[None, :] < e[:, None]).astype(np.float32).reshape(1, -1), (P, ER * ER))
    pick = np.zeros((32, ER, P), np.float32)
    for k in range(ER):
        pick[ES + k, k] = pick[16 + ES + k, k] = 1.0
    return {"rel": rel, "ident": np.eye(P, dtype=np.float32), "earlier": np.ascontiguousarray(earlier),
            "pick": pick.reshape(32, ER * P)}


def kernel(**inputs):
    import numpy as np
    import concourse.bacc as bacc
    from concourse import mybir as mb
    from concourse.bass_utils import run_bass_kernel_spmd

    nc = bacc.Bacc("TRN2", target_bir_lowering=False, num_devices=1)
    arrays, aps = {}, {}
    for name, arr in [(n, inputs[n]) for n in _INS] + list(shape_constants().items()):
        arr = np.ascontiguousarray(arr)
        arrays[f"in_{name}"] = arr
        aps[name] = nc.dram_tensor(f"in_{name}", arr.shape, mb.dt.from_np(arr.dtype), kind="ExternalInput").ap()
    out = nc.dram_tensor("out_dram", (B, N, C), mb.dt.float32, kind="ExternalOutput").ap()
    decoder_block(nc, aps, out)
    r = run_bass_kernel_spmd(nc, [arrays], core_ids=[0])
    return r.results[0]["out_dram"]
```

```python
import concourse.bass as bass
from concourse import mybir
from contextlib import ExitStack

F32 = mybir.dt.float32
F32R = mybir.dt.float32r
I32 = mybir.dt.int32
ALU = mybir.AluOpType
ACT = mybir.ActivationFunctionType
AXIS = mybir.AxisListType

B, N, C = 2, 512, 128
HEADS, DH = 16, 64
S2 = 77
HID, ES, ER = 512, 2, 8
P = 128
NT = N // P
PAIRS = HEADS // 2
UNITS = B * PAIRS
KC = HID // P
E = ES + ER
CHUNKS = E * KC
SCALE = DH ** -0.5
XSCALE = float(C) ** -0.5
LN_EPS = 1e-5
RMS_EPS = 1.1920928955078125e-07
NEG = 1e30
BIG = 3e38
SLOPES = [(2.0 ** (-2.0 ** (-(4 - 3)))) ** (h + 1) for h in range(HEADS)]
BANKS = 6
ROW_AT = [sum(P * (k + 1) for k in range(i)) for i in range(NT)]
HEAD_COLS = ROW_AT[-1] + P * NT
GROUPS = [[0], [1, 3], [2]]
GROUP_AT = [0, 512, 1024]
KEY_AT = [0, 512, 1024, 896]
FFN_SLOTS = 3
FFN_BUFS = 4
WARM = (6, 6, 4)
SPLIT_AT = 7.0
ALIBI_AFTER = "N2"
GATE_B_AT = 1.5
DVE_HI = ((1, 0),)
POOL_NORMS = (2,)
GATED_AT = 0.7
LAG = 3


PE_ROUND = "S1 S0 S2 S3 TB0 TA2 YB TA0 TA1 TB2 Q TB1 X2 K OA X3 X OB YA".split()
ACT_ROUND = "S1 S0 TB0 TA2 TA0 TA1 TB2 Q TB1 S2 X2 K X3 OA X OB S3".split()
DVE_ROUND = "S1 R3 N3 S0 S2 S3 TA2 R1 TB0 TA0 TA1 TB2 N1 TB1 Q R2 X2 R0 K N2 N0 X3 X".split()


def round_steps(token, u, extra):
    if token[0] == "X":
        return extra.get(token, [])
    i = "AB".find(token[1:2])
    kind, steps = {
        "S": (u, lambda v: [("score", (v, int(token[1]), j)) for j in range(2)]),
        "R": (u - (token == "R3"), lambda v: [("recip", (v, int(token[1])))]),
        "N": (u - (token == "N3"), lambda v: [("pool_norm" if int(token[1]) in POOL_NORMS else "norm",
                                         (v, int(token[1])))]),
        "Q": (u + 1, lambda v: [("projQ", (v,))]),
        "K": (u + 1, lambda v: [("projK", (v,))]),
        "B": (u + 2, lambda v: [("alibi", (v,))]),
        "T": (u - 1, lambda v: [("probT", (v, i, int(token[2])))]),
        "O": (u - 1, lambda v: [("attn", (v, i))]),
        "Y": (u - 1 - i, lambda v: [("outproj", (v, i))]),
    }[token[0]]
    return steps(kind) if 0 <= kind < UNITS else []


CHAIN_PLACE = {"yT": (None, 0, None, None), "res1": (1, None, 1, 1), "x1": (None, None, 2, None),
               "x1T": (5, 5, None, None), "xq": (6, 6, None, None), "xscore": (7, None, 7, None),
               "xexp": (None, 8, None, None), "xprob": (None, None, 8, None), "xpT": (11, 11, None, None),
               "xout": (11, None, 11, 11), "x2": (None, None, 12, 12), "xr": (None, None, 14, None),
               "x2T": (14, 15, None, None), "logit": (15, 15, None, None), "gates": (None, None, 15, None),
               "xnT": (17, 17, 17, None), "gatesT": (18, 18, None, None)}

CHAIN_AT = {"yT": (None, 8, None, None), "res1": (10, None, 9, 9), "x1": (None, None, 11.5, None),
            "x1T": (14.7, 14.2, None, None), "xq": (16, 16, None, None), "xscore": (18, None, 17, None),
            "xexp": (None, 20, None, None), "xprob": (None, None, 20, None), "xpT": (23.0, 22.7, None, None),
            "xout": (25, None, 24, 24), "x2": (None, None, 27.5, 27.5), "x2T": (29.8, 29.5, None, None),
            "xr": (None, None, 29.5, None), "logit": (31.8, 31.6, None, None), "xnT": (35, 36, 36, None),
            "gates": (None, None, 31.5, None), "gatesT": (39, 39, None, None)}


def build_schedules():
    head = [("xT", (0,)), ("split_wqkv", (0,)), ("split_wqkv", (2,)), ("projQ", (0,)), ("projK", (0,)),
            ("alibi", (0,))]
    orders = [list(head) for _ in range(4)]
    for order in orders[1:3]:
        order[0:2] = order[1::-1]
    for u in range(UNITS):
        extra = {"X": [], "X2": [], "X3": []}
        first, second, third = [t for t in PE_ROUND if t in extra]
        if u == 0:
            extra[first] = [("cols", ())]
            extra[second] = [("V", (0, 0, t)) for t in range(NT)]
            extra[third] = [("V", (0, 1, t)) for t in range(NT)]
        elif u == 2:
            extra[first], extra[second], extra[third] = [("xT", (1,))], [("split_wqkv", (1,))], [("split_wqkv", (3,))]
        elif u == 1:
            extra[first], extra[second], extra[third] = [("ctxT", ())], [("ctxK", ())], [("ctxV", ())]
        elif 5 <= u <= 12:
            extra["X"] = [("V", (1, (u - 5) // NT, (u - 5) % NT))]
        if u == UNITS - 1:
            extra[first] = extra[first] + [("split_ffn", (0,))]
            extra[second] = extra[second] + [("split_ffn", (1,))]
            extra[third] = extra[third] + [("split_ffn", (2,))]
        pool_round = [t for t in DVE_ROUND for t in ((t, "B") if t == ALIBI_AFTER else (t,))]
        for lane, tokens in enumerate((PE_ROUND, ACT_ROUND, DVE_ROUND, pool_round)):
            for token in tokens:
                if u == 0 and token in ("TA0", "TA1"):
                    orders[lane].append(("split_wqkv", (4 + (token == "TA1"),)))
                if u == 0 and token == "TB1":
                    orders[lane].append(("alibi", (1,)))
                orders[lane] += round_steps(token, u, extra)
                if token in extra and u > PAIRS:
                    at = (u - PAIRS - 1) * 3 + (first, second, third).index(token) - 1
                    orders[lane] += [(k, (0,)) for k, p in CHAIN_PLACE.items() if p[lane] == at]

    timed = [[] for _ in range(4)]

    def put(step, *at):
        for lane, t in zip(timed, at):
            if t is not None:
                lane.append((t, step))

    last = UNITS - 1
    put(("recip", (last, NT - 1)), None, None, -2)
    put(("pool_norm" if NT - 1 in POOL_NORMS else "norm", (last, NT - 1)), None, None, -1, -1)
    put(("outproj", (last - 1, 1)), 0.1)
    for j in range(2):
        for n in range(3):
            t = 0.5 + j + n / 10
            put(("probT", (last, j, n)), t, t, t)
        put(("attn", (last, j)), 3.6 + j, 3.6 + j, 2.6 + j)
        put(("outproj", (last, j)), 6.1 + j)
    for kind, at in CHAIN_AT.items():
        put((kind, (1,)), *at)
    for c in range(B * CHUNKS):
        b, cb = divmod(c, CHUNKS)
        e, k = divmod(cb, KC)
        if k == 0 and e >= ES:
            put(("gate_b", (b, e)), c + GATE_B_AT, c + GATE_B_AT + 0.5)
        put(("up", (b, cb)), c, c, c)
        put(("down", (b, cb)), c + LAG + 0.5)
        if k == KC - 1 and e >= ES - 1:
            put(("gated", (b, e)), None, None, c + LAG + GATED_AT, c + LAG + GATED_AT)
    for w in range(FFN_SLOTS, B * E):
        put(("split_ffn", (w,)), None, None, KC * w - SPLIT_AT, KC * w - SPLIT_AT)
    for b, t in ((0, CHUNKS + LAG + 5), (1, B * CHUNKS + LAG + 1)):
        put(("most", (b,)), t - 1, None, t - 1)
        put(("final", (b,)), t, None, t, t)
        put(("store", (b,)), None, t + 5, t + 1.5)
    for order, lane in zip(orders, timed):
        order += [step for _, step in sorted(lane, key=lambda x: x[0])]
    return orders


LAST_READER = {"xT": "dve", "projQ": "dve", "projK": "dve", "V": "dve", "score": "dve", "cols": "dve",
               "ctxT": "act", "ctxK": "act", "ctxV": "dve", "probT": "dve", "attn": "act", "res1": "dve",
               "x1T": "act", "xq": "act", "xscore": "dve", "xpT": "act", "xout": "dve", "x2T": "act",
               "logit": "act", "xnT": "dve", "gatesT": "act", "gate_b": "act", "up": "dve", "most": "dve",
               "final": "dve"}
PE_KINDS = list(LAST_READER) + ["outproj", "down"]
ACT_KINDS = ["xT", "split_wqkv", "projQ", "projK", "V", "score", "ctxT", "ctxK", "probT", "attn", "yT",
             "x1T", "xq", "xexp", "xpT", "x2T", "logit", "xnT", "gatesT", "gate_b", "gelu",
             "up"]
DVE_KINDS = ["xT", "split_wqkv", "projQ", "projK", "V", "score", "recip", "norm", "cols", "ctxV", "probT", "res1", "x1",
             "xscore", "xprob", "xout", "x2", "xr", "xnT", "gates", "up", "gated", "most", "final", "store", "link", "mask",
             "split_ffn"]
POOL_KINDS = ["alibi", "pool_norm", "split_wqkv", "split_ffn", "res1", "xout", "x2", "gated", "final", "pool_link"]


def decoder_block(nc, a, out):
    PE_STEPS, ACT_STEPS, DVE_STEPS, POOL_STEPS = build_schedules()
    ring = [st for st in PE_STEPS if st[0] in LAST_READER]
    ring_of = {st: n for n, st in enumerate(ring)}

    def counts(steps):
        seen, out_ = {}, {}
        for st in steps:
            seen[st[0]] = seen.get(st[0], 0) + 1
            out_[st] = seen[st[0]]
        return out_

    pe_count, act_count = counts(PE_STEPS), counts(ACT_STEPS)
    dve_count, pool_count = counts(DVE_STEPS), counts(POOL_STEPS)

    def all_of(count, kind, args):
        return max(count[(kind, g)] for g in args)

    with ExitStack() as ctx:
        def sb(name, shape, dt=F32):
            return ctx.enter_context(nc.sbuf_tensor(name, shape, dt))

        rel = sb("rel", [P, N])
        ident = sb("ident", [P, P])
        earlier = sb("earlier", [P, ER * ER])
        pick = sb("pick", [32, ER * P], F32R)
        x_tok = sb("x_tok", [P, B * NT, C])
        xT_hi, xT_lo = sb("xT_hi", [P, B * N], F32R), sb("xT_lo", [P, B * N], F32R)
        stage = sb("stage", [P, 3 * HEADS * DH])
        pick_f = stage[0:32, 2 * HEADS * DH:3 * HEADS * DH]
        wq_hi, wq_lo = sb("wq_hi", [P, 3 * HEADS * DH], F32R), sb("wq_lo", [P, 3 * HEADS * DH], F32R)
        wo = sb("wo", [P, HEADS, C])
        bias = sb("bias", [P, 4, N])
        q_hi, q_lo = sb("q_hi", [P, 2, N], F32R), sb("q_lo", [P, 2, N], F32R)
        k_hi, k_lo = sb("k_hi", [P, 2, N], F32R), sb("k_lo", [P, 2, N], F32R)
        v_hl = sb("v_hl", [P, NT, HEADS, 2 * DH], F32R)
        prob = sb("prob", [P, 2, 2 * HEAD_COLS])
        pT_hi, pT_lo = sb("pT_hi", [P, 2 * HEAD_COLS], F32R), sb("pT_lo", [P, 2 * HEAD_COLS], F32R)
        o_sb = sb("o_sb", [P, 2, N])
        negmax, expsum, recip = sb("negmax", [P, 2, 8]), sb("expsum", [P, 2, 8]), sb("recip", [P, 2, 8])
        NROWS = E * KC + 5
        vec_rows, vec = sb("vec_rows", [NROWS, P]), sb("vec", [P, NROWS])
        B1, BOUT, BQ, BK, GS, GR = 0, E * KC, E * KC + 1, E * KC + 2, E * KC + 3, E * KC + 4
        wxq, wxk, wxv = sb("wxq", [P, C]), sb("wxk", [P, C]), sb("wxv", [P, C])
        ctx_tok, ctx_T = sb("ctx_tok", [S2, B, C]), sb("ctx_T", [P, B, S2])
        ctx_k, ctx_v = sb("ctx_k", [P, B, S2]), sb("ctx_v", [S2, B, C])
        bv_row = sb("bv_row", [S2, C])
        mask_i, keep, shut = sb("mask_i", [P, B, S2], I32), sb("keep", [P, B, S2]), sb("shut", [P, B, S2])
        yT_sb = sb("yT_sb", [P, N])
        xr_tok = yT_sb[:, :].rearrange("p (t c) -> p t c", t=NT)
        r_tok = sb("r_tok", [P, NT, C])
        x1_tok = sb("x1_tok", [P, NT, C])
        xT_sb = sb("xT_sb", [P, N])
        qx_sb = sb("qx_sb", [P, N])
        xs = sb("xs", [P, NT, S2])
        xsT = sb("xsT", [S2, N])
        small = sb("small", [P, 64])
        stats, mv = sb("stats", [P, NT, 6]), sb("mv", [P, NT, 2])
        x2_tok = sb("x2_tok", [P, B * NT, C])
        cent = sb("cent", [P, ER])
        b2 = sb("b2", [32, C])
        ez, sg = sb("ez", [P, NT, ER]), sb("sg", [P, NT, ER])
        cmp1, cmp2 = (qx_sb[:, i * 256:(i + 1) * 256].rearrange("p (a j) -> p a j", j=ER) for i in range(2))
        gates, gates_hl = sb("gates", [P, NT, ER]), sb("gates_hl", [P, NT, 32])
        g_hi = sb("g_hi", [P, NT, ER], F32R)
        gatesT = sb("gatesT", [32, B, N], F32R)
        gate_b = bias

        def ffn_buf(n):
            hi, lo = ((q_hi, k_hi), (q_lo, k_lo))[n % FFN_BUFS // 2]
            return hi[:, n % 2, :], lo[:, n % 2, :]
        acc = prob[:, 0, 0:B * N]
        part = prob[:, 1, 0:2 * N]
        out_tok = r_tok

        ring_bank = [ctx.enter_context(nc.psum_tensor(f"ring{i}", [P, 512], F32)) for i in range(BANKS)]
        sum_bank = [ctx.enter_context(nc.psum_tensor(f"sum{i}", [P, 512], F32)) for i in range(2)]

        def sem(name):
            return ctx.enter_context(nc.semaphore(name))

        filled = {k: sem(f"filled_{k}") for k in PE_KINDS}
        act_done = {k: sem(f"act_done_{k}") for k in ACT_KINDS}
        dve_done = {k: sem(f"dve_done_{k}") for k in DVE_KINDS}
        pool_done = {k: sem(f"pool_done_{k}") for k in POOL_KINDS}
        LOADS = ["ident", "rel", "x0", "x1", "wq", "wk", "wqk", "wv", "wout", "vecs", "xw", "ctx", "tail"]
        loaded = {k: sem(f"loaded_{k}") for k in LOADS}
        ffn_loaded = [sem(f"ffn_loaded_{i}") for i in range(FFN_SLOTS)]
        stored = sem("stored")
        block = ctx.enter_context(nc.Block())

        def bank(st):
            return ring_bank[ring_of[st] % BANKS]

        def released(st):
            if LAST_READER[st[0]] == "act":
                return act_done[st[0]], act_count[st]
            return dve_done[st[0]], dve_count[st]

        def ffn_w(w):
            at = (w % FFN_SLOTS) * 2 * HID
            return at, at + HID

        def xn(b, kind):
            if b == 0:
                return xT_hi[:, kind * N:(kind + 1) * N], xT_lo[:, kind * N:(kind + 1) * N]
            flat = v_hl[:, :, :, :].rearrange("p t h d -> p (t h d)")
            return (flat[:, 2 * kind * N:(2 * kind + 1) * N], flat[:, (2 * kind + 1) * N:(2 * kind + 2) * N])

        def dve_splits(b, c):
            return (b, c % KC) in DVE_HI

        up_copies, n = {}, 0
        for b, c in [(b, c) for b in range(B) for c in range(CHUNKS)]:
            n += not dve_splits(b, c)
            up_copies[(b, c)] = n

        def pool_adds(i):
            return i - i // ER

        def y_index(b, e):
            return b * (ER + 1) + max(e - ES + 1, 0)

        @block.sync
        def _(sp):
            x_v = a["x"].rearrange("b (t p) c -> b p t c", p=P)
            sp.dma_start(x_tok[:, 0:NT, :], x_v[0]).then_inc(loaded["x0"], 16)
            w_qkv = a["L0_attn_w_qkv"]
            for n, lo, hi in (("wq", 0, 512), ("wk", 1024, 1536)):
                sp.dma_start(stage[:, lo:hi], w_qkv[:, lo:hi]).then_inc(loaded[n], 16)
            sp.dma_start(rel[:, :], a["rel"]).then_inc(loaded["rel"], 16)
            for n, lo, hi in (("wv", 2048, 3072), ("wqk", 512, 1024), ("wqk", 1536, 2048)):
                sp.dma_start(stage[:, lo:hi], w_qkv[:, lo:hi]).then_inc(loaded[n], 16)
            sp.dma_start(x_tok[:, NT:2 * NT, :], x_v[1]).then_inc(loaded["x1"], 16)
            wo_v = a["L0_attn_w_out"].rearrange("(h d) c -> d h c", d=DH)
            for half in range(2):
                sp.dma_start(wo[half * DH:(half + 1) * DH, :, :], wo_v).then_inc(loaded["wout"], 16)
            at = 0
            for n, rows in (("L0_ffn_b1_s", ES * KC), ("L0_ffn_b1_r", ER * KC)):
                sp.dma_start(vec_rows[at:at + rows, :],
                             a[n].rearrange("e (k p) -> (e k) p", p=P)).then_inc(loaded["vecs"], 16)
                at += rows
            for n in ("L0_attn_b_out", "L0_xattn_bq", "L0_xattn_bk", "L0_ffn_g_shared", "L0_ffn_g_routed"):
                sp.dma_start(vec_rows[at:at + 1, :],
                             a[n].rearrange("(a c) -> a c", a=1)).then_inc(loaded["vecs"], 16)
                at += 1
            sp.dma_start(ctx_tok[:, :, :], a["ctx_1024"].rearrange("b s c -> s b c")).then_inc(loaded["ctx"], 16)
            for t, n in ((wxq, "Wq"), (wxk, "Wk"), (wxv, "Wv")):
                sp.dma_start(t[:, :], a["L0_xattn_" + n]).then_inc(loaded["xw"], 16)
            sp.dma_start(bv_row[:, :], a["L0_xattn_bv"].partition_broadcast(S2)).then_inc(loaded["xw"], 16)
            sp.dma_start(mask_i[:, :, :], a["mask_BxS2_if1"].partition_broadcast(P)).then_inc(loaded["tail"], 16)
            sp.dma_start(cent[:, :], a["L0_ffn_centroids"]).then_inc(loaded["tail"], 16)
            for at in (0, 16):
                sp.wait_ge(dve_done["link"], 2)
                sp.dma_start(b2[at:at + ES, :], a["L0_ffn_b2_s"]).then_inc(loaded["tail"], 16)
                sp.dma_start(b2[at + ES:at + E, :], a["L0_ffn_b2_r"]).then_inc(loaded["tail"], 16)
            sp.dma_start(earlier[:, :], a["earlier"]).then_inc(loaded["tail"], 16)
            sp.wait_ge(pool_done["split_wqkv"], 2)
            sp.dma_start(pick_f, a["pick"]).then_inc(loaded["tail"], 16)
            sp.wait_ge(pool_done["split_wqkv"], 4)
            for w in range(B * E):
                b, e = divmod(w, E)
                if w == FFN_SLOTS - 1:
                    sp.wait_ge(dve_done["mask"], 2)
                if w >= FFN_SLOTS:
                    sp.wait_ge(pool_done["split_ffn"], w - FFN_SLOTS + 1)
                s, i = ("s", e) if e < ES else ("r", e - ES)
                at = ffn_w(w)[0]
                sp.dma_start(stage[:, at:at + HID], a["L0_ffn_W1_" + s][i]).then_inc(ffn_loaded[w % FFN_SLOTS], 16)
                sp.dma_start(stage[:, at + HID:at + 2 * HID].rearrange("p (k c) -> p k c", k=KC),
                             a["L0_ffn_W2_" + s][i].rearrange("(k p) c -> p k c", p=P)).then_inc(ffn_loaded[w % FFN_SLOTS], 16)

        @block.tensor
        def _(pe):

            def split3(dst, lhs_hi, lhs_lo, rhs_hi, rhs_lo, first=True, last=True):
                pe.matmul(dst, lhs_hi, rhs_hi, start=first, stop=False)
                pe.matmul(dst, lhs_lo, rhs_hi, start=False, stop=False)
                return pe.matmul(dst, lhs_hi, rhs_lo, start=False, stop=last)

            def keep_warm(n):
                for _ in range(n):
                    pe.matmul(sum_bank[1][:, 0:P], o_sb[:, 0, 0:P], o_sb[:, 0, 0:P], start=True, stop=True)

            def turn(dst, src, p):
                return pe.transpose(dst, src, ident[0:p, 0:p])

            first_out = [min(pe_count[("outproj", (b * PAIRS + p, j))] for p in range(PAIRS) for j in range(2))
                         for b in range(B)]
            pe.wait_ge(dve_done["link"], 1)
            keep_warm(WARM[0])
            for st in PE_STEPS:
                kind, g = st
                if kind in LAST_READER:
                    n = ring_of[st]
                    if kind == "score" and g[2] == 1:
                        continue
                    upto = n + 1 if kind == "score" else n
                    for m in range(n, upto + 1):
                        if m >= BANKS:
                            done, count = released(ring[m - BANKS])
                            pe.wait_ge(done, count)
                    ps = bank(st)
                if kind == "xT":
                    b, = g
                    pe.wait_ge(loaded["ident"], 16)
                    pe.wait_ge(loaded[f"x{b}"], 16)
                    for t in range(NT):
                        mm = turn(ps[:, t * P:(t + 1) * P], x_tok[:, b * NT + t, :], P)
                elif kind in ("projQ", "projK"):
                    u, = g
                    b, p = divmod(u, PAIRS)
                    i = kind == "projK"
                    pe.wait_ge(dve_done["xT"], b + 1)
                    if p < 4:
                        pe.wait_ge(dve_done["split_wqkv"], 1 + i)
                    else:
                        pe.wait_ge(pool_done["split_wqkv"], 3 + i)
                    at = i * HEADS * DH + p * P
                    mm = split3(ps[:, :], wq_hi[:, at:at + P], wq_lo[:, at:at + P],
                                xT_hi[:, b * N:(b + 1) * N], xT_lo[:, b * N:(b + 1) * N])
                elif kind == "V":
                    b, half, t = g
                    pe.wait_ge(dve_done["xT"], b + 1)
                    pe.wait_ge(pool_done["split_wqkv"], 1 + half)
                    at, tk = 2 * HEADS * DH + half * 512, b * N + t * P
                    mm = split3(ps[:, :], xT_hi[:, tk:tk + P], xT_lo[:, tk:tk + P],
                                wq_hi[:, at:at + 512], wq_lo[:, at:at + 512])
                elif kind == "score":
                    u, i, _ = g
                    pe.wait_ge(dve_done["projQ"], u + 1)
                    pe.wait_ge(dve_done["projK"], u + 1)
                    s, w = u % 2, P * (i + 1)
                    for n3, (l, r) in enumerate(((q_hi, k_hi), (q_lo, k_hi), (q_hi, k_lo))):
                        for j in range(2):
                            rows = slice(j * DH, (j + 1) * DH)
                            dst = ring_bank[(ring_of[st] + j) % BANKS]
                            mm = pe.matmul(dst[:, 0:w], l[rows, s, i * P:(i + 1) * P], r[rows, s, 0:w],
                                           start=n3 == 0, stop=n3 == 2)
                            if n3 == 2:
                                mm.then_inc(filled["score"], 1)
                    continue
                elif kind == "probT":
                    u, j, grp = g
                    dve_norms = [(u, i) for i in range(NT) if i not in POOL_NORMS]
                    pe.wait_ge(dve_done["norm"], all_of(dve_count, "norm", dve_norms))
                    pe.wait_ge(pool_done["pool_norm"], all_of(pool_count, "pool_norm", [(u, i) for i in POOL_NORMS]))
                    for kt in GROUPS[grp]:
                        for i in range(kt, NT):
                            src = j * HEAD_COLS + ROW_AT[i] + kt * P
                            dst = KEY_AT[kt] - GROUP_AT[grp] + (i - kt) * P
                            mm = turn(ps[:, dst:dst + P], prob[:, u % 2, src:src + P], P)
                elif kind == "attn":
                    u, j = g
                    b, p = divmod(u, PAIRS)
                    h = 2 * p + j
                    pe.wait_ge(dve_done["probT"], all_of(dve_count, "probT", [(u, j, n) for n in range(3)]))
                    pe.wait_ge(dve_done["V"], 8 * b + 4 * (h // 8) + 4)
                    for kt in range(NT):
                        w = N - kt * P
                        at = j * HEAD_COLS + KEY_AT[kt]
                        for n2, pt in enumerate((pT_hi, pT_lo)):
                            mm = pe.matmul(ps[:, kt * P:N], v_hl[:, kt, h, :], pt[:, at:at + w],
                                           start=kt == 0 and n2 == 0, stop=kt == NT - 1 and n2 == 1)
                elif kind == "outproj":
                    u, j = g
                    b, p = divmod(u, PAIRS)
                    h = 2 * p + j
                    pe.wait_ge(act_done["attn"], act_count[("attn", (u, j))])
                    pe.wait_ge(loaded["wout"], 32)
                    mm = pe.matmul(sum_bank[b][:, :], wo[:, h, :], o_sb[:, j, :], start=pe_count[st] == first_out[b],
                                   stop=pe_count[st] == first_out[b] + HEADS - 1)
                elif kind == "cols":
                    pe.wait_ge(loaded["vecs"], 16 * 7)
                    mm = turn(ps[:, 0:NROWS], vec_rows[:, :], NROWS)
                elif kind == "ctxT":
                    pe.wait_ge(loaded["ctx"], 16)
                    for b in range(B):
                        mm = turn(ps[:, b * P:b * P + S2], ctx_tok[:, b, :], S2)
                elif kind == "ctxK":
                    pe.wait_ge(act_done["ctxT"], 1)
                    pe.wait_ge(loaded["xw"], 64)
                    mm = pe.matmul(ps[:, 0:B * S2], wxk[:, :], ctx_T[:, :, :].rearrange("p b s -> p (b s)"),
                                   start=True, stop=True)
                elif kind == "ctxV":
                    for b in range(B):
                        mm = pe.matmul(ps[0:S2, b * C:(b + 1) * C], ctx_T[:, b, :], wxv[:, :], start=True, stop=True)
                elif kind == "res1":
                    b, = g
                    pe.wait_ge(act_done["yT"], b + 1)
                    for t in range(NT):
                        mm = turn(ps[:, t * P:(t + 1) * P], yT_sb[:, t * P:(t + 1) * P], P)
                elif kind == "x1T":
                    b, = g
                    pe.wait_ge(dve_done["x1"], b + 1)
                    for t in range(NT):
                        mm = turn(ps[:, t * P:(t + 1) * P], x1_tok[:, t, :], P)
                elif kind == "xq":
                    b, = g
                    pe.wait_ge(act_done["x1T"], b + 1)
                    mm = pe.matmul(ps[:, :], wxq[:, :], xT_sb[:, :], start=True, stop=True)
                elif kind == "xscore":
                    b, = g
                    pe.wait_ge(act_done["xq"], b + 1)
                    pe.wait_ge(act_done["ctxK"], 1)
                    for t in range(NT):
                        mm = pe.matmul(ps[:, t * P:t * P + S2], qx_sb[:, t * P:(t + 1) * P], ctx_k[:, b, :],
                                       start=True, stop=True)
                elif kind == "xpT":
                    b, = g
                    pe.wait_ge(dve_done["xprob"], b + 1)
                    for t in range(NT):
                        mm = turn(ps[0:S2, t * P:(t + 1) * P], xs[:, t, :], P)
                elif kind == "xout":
                    b, = g
                    pe.wait_ge(act_done["xpT"], b + 1)
                    pe.wait_ge(dve_done["ctxV"], 1)
                    for t in range(NT):
                        mm = pe.matmul(ps[:, t * P:(t + 1) * P], xsT[:, t * P:(t + 1) * P], ctx_v[:, b, :],
                                       start=True, stop=True)
                elif kind == "x2T":
                    b, = g
                    pe.wait_ge(dve_done["x2"], 2 * b + 1)
                    for t in range(NT):
                        mm = turn(ps[:, t * P:(t + 1) * P], x2_tok[:, b * NT + t, :], P)
                elif kind == "logit":
                    b, = g
                    pe.wait_ge(act_done["x2T"], b + 1)
                    pe.wait_ge(loaded["tail"], 16 * 8)
                    for t in range(NT):
                        mm = pe.matmul(ps[:, t * ER:(t + 1) * ER], xT_sb[:, t * P:(t + 1) * P], cent[:, :],
                                       start=True, stop=True)
                elif kind == "xnT":
                    b, = g
                    pe.wait_ge(dve_done["xr"], b + 1)
                    for t in range(NT):
                        mm = turn(ps[:, t * P:(t + 1) * P], xr_tok[:, t, :], P)
                elif kind == "gatesT":
                    b, = g
                    pe.wait_ge(dve_done["gates"], b + 1)
                    for t in range(NT):
                        mm = turn(ps[0:32, t * P:(t + 1) * P], gates_hl[:, t, :], P)
                elif kind == "gate_b":
                    b, e = g
                    pe.wait_ge(act_done["gatesT"], b + 1)
                    pe.wait_ge(dve_done["mask"], 2)
                    mm = pe.matmul(ps[:, :], pick[:, (e - ES) * P:(e - ES + 1) * P], gatesT[:, b, :],
                                   start=True, stop=True)
                elif kind == "up":
                    b, c = g
                    e, k = divmod(c, KC)
                    pe.wait_ge(dve_done["xnT"], b + 1)
                    pe.wait_ge(pool_done["split_ffn"], b * E + e + 1)
                    x_hi, x_lo = xn(b, int(e >= ES))
                    at = ffn_w(b * E + e)[0] + k * P
                    mm = split3(ps[:, :], wq_hi[:, at:at + P], wq_lo[:, at:at + P], x_hi, x_lo)
                elif kind == "down":
                    b, c = g
                    e, k = divmod(c, KC)
                    m = y_index(b, e)
                    first = k == 0 and e in (0, *range(ES, E))
                    last = k == KC - 1 and e >= ES - 1
                    dst = sum_bank[m % 2][:, :]
                    if first and m < 2:
                        pe.wait_ge(act_done["yT"], m + 1)
                    elif first:
                        pe.wait_ge(dve_done["gated"], m - 1)
                    if first and e == 0:
                        pe.wait_ge(act_done["gatesT"], b + 1)
                        pe.wait_ge(loaded["tail"], 16 * 8)
                        pe.matmul(dst, b2[:, :], gatesT[:, b, :].bitcast(F32), start=True, stop=False)
                    pe.wait_ge(dve_done["up"], dve_count[("up", (b, c))])
                    at = ffn_w(b * E + e)[1] + k * P
                    hi, lo = ffn_buf(b * CHUNKS + c)
                    mm = split3(dst, wq_hi[:, at:at + P], wq_lo[:, at:at + P], hi, lo, first=first and e != 0, last=last)
                elif kind == "most":
                    b, = g
                    pe.wait_ge(pool_done["gated"], (b + 1) * (ER - 1))
                    for t in range(NT):
                        mm = turn(ps[:, t * P:(t + 1) * P], acc[:, b * N + t * P:b * N + (t + 1) * P], P)
                elif kind == "final":
                    b, = g
                    i = (b + 1) * ER - 1
                    pe.wait_ge(dve_done["gated"], y_index(b, E - 1) + 1)
                    for t in range(NT):
                        at = (i % 2) * N + t * P
                        mm = turn(ps[:, t * P:(t + 1) * P], part[:, at:at + P], P)
                else:
                    continue
                mm.then_inc(filled[kind], 1)
                if st in (("xT", (0,)), ("projK", (0,))):
                    keep_warm(WARM[1 + (kind == "projK")])

        @block.scalar
        def _(act):

            def copy(dst, src, scale=1.0):
                return act.activation(dst, src, ACT.Copy, scale=scale)

            act.dma_start(ident[:, :], a["ident"]).then_inc(loaded["ident"], 16)
            for st in ACT_STEPS:
                kind, g = st
                if kind in LAST_READER and kind in ACT_KINDS and kind != "score":
                    act.wait_ge(filled[kind], pe_count[st])
                    ps = bank(st)
                if kind == "xT":
                    b, = g
                    op = copy(xT_hi[:, b * N:(b + 1) * N], ps[:, :])
                elif kind == "split_wqkv":
                    n, = g
                    act.wait_ge(loaded[("wq", "wqk", "wk", "wqk", "wv", "wv")[n]], 32 if n in (1, 3) else 16)
                    op = copy(wq_hi[:, n * 512:(n + 1) * 512], stage[:, n * 512:(n + 1) * 512])
                elif kind in ("projQ", "projK"):
                    u, = g
                    if u >= 2:
                        act.wait_ge(filled["score"], 8 * (u - 1))
                    dst, scale = (q_hi, SCALE) if kind == "projQ" else (k_hi, 1.0)
                    op = copy(dst[:, u % 2, :], ps[:, :], scale)
                elif kind == "V":
                    b, half, t = g
                    if b == 1:
                        heads = [(4 * half + n, j) for n in range(4) for j in range(2)]
                        act.wait_ge(filled["attn"], all_of(pe_count, "attn", heads))
                    op = copy(v_hl[:, t, 8 * half:8 * half + 8, 0:DH], ps[:, :].rearrange("p (h d) -> p h d", d=DH))
                elif kind == "score":
                    u, i, j = g
                    s, w = u % 2, P * (i + 1)
                    at = j * HEAD_COLS + ROW_AT[i]
                    act.wait_ge(dve_done["score"], dve_count[st])
                    op = act.activation(prob[:, s, at:at + w], prob[:, s, at:at + w], ACT.Exp, scale=-1.0,
                                        bias=negmax[:, s, 2 * i + j:2 * i + j + 1],
                                        accum_out=expsum[:, s, 2 * i + j:2 * i + j + 1])
                elif kind == "probT":
                    u, j, grp = g
                    w = 256 if grp == 2 else 512
                    at = j * HEAD_COLS + GROUP_AT[grp]
                    if u >= 1:
                        act.wait_ge(filled["attn"], pe_count[("attn", (u - 1, j))])
                    op = copy(pT_hi[:, at:at + w], ps[:, 0:w])
                elif kind == "attn":
                    u, j = g
                    if u >= 1:
                        act.wait_ge(filled["outproj"], pe_count[("outproj", (u - 1, j))])
                    op = copy(o_sb[:, j, :], ps[:, :])
                elif kind == "ctxT":
                    op = copy(ctx_T[:, :, :], ps[:, 0:B * P].rearrange("p (b s) -> p b s", b=B)[:, :, 0:S2])
                elif kind == "ctxK":
                    act.wait_ge(dve_done["cols"], 1)
                    op = act.activation(ctx_k[:, :, :], ps[:, 0:B * S2].rearrange("p (b s) -> p b s", b=B), ACT.Identity,
                                   bias=vec[:, BK:BK + 1])
                elif kind == "yT":
                    b, = g
                    heads = [(b * PAIRS + p, j) for p in range(PAIRS) for j in range(2)]
                    act.wait_ge(filled["outproj"], all_of(pe_count, "outproj", heads))
                    act.wait_ge(dve_done["cols"], 1)
                    op = act.activation(yT_sb[:, :], sum_bank[b][:, :], ACT.Identity, bias=vec[:, BOUT:BOUT + 1])
                elif kind == "x1T":
                    op = copy(xT_sb[:, :], ps[:, :])
                elif kind == "xq":
                    op = act.activation(qx_sb[:, :], ps[:, :], ACT.Identity, bias=vec[:, BQ:BQ + 1])
                elif kind == "xexp":
                    b, = g
                    act.wait_ge(dve_done["xscore"], b + 1)
                    op = act.activation(xs[:, :, :], xs[:, :, :], ACT.Exp)
                elif kind == "xpT":
                    op = copy(xsT[:, :], ps[0:S2, :])
                elif kind == "x2T":
                    op = copy(xT_sb[:, :], ps[:, :])
                elif kind == "logit":
                    op = act.activation(ez[:, :, :].rearrange("p t e -> p (t e)"), ps[:, 0:NT * ER], ACT.Exp, scale=-1.0)
                elif kind == "xnT":
                    b, = g
                    if b == 0:
                        act.wait_ge(filled["projK"], UNITS)
                        act.wait_ge(filled["V"], 8 * B)
                    else:
                        act.wait_ge(filled["attn"], 2 * UNITS)
                    act.activation(xn(b, 0)[0], ps[:, :], ACT.Copy, scale=vec[:, GS:GS + 1])
                    op = act.activation(xn(b, 1)[0], ps[:, :], ACT.Copy, scale=vec[:, GR:GR + 1])
                elif kind == "gatesT":
                    b, = g
                    op = copy(gatesT[:, b, :], ps[0:32, :])
                elif kind == "gate_b":
                    b, e = g
                    m = b * ER + e - ES
                    if m >= 2:
                        pb, pe = divmod(m - 2, ER)
                        act.wait_ge(dve_done["gated"], y_index(pb, ES + pe) + 1)
                    else:
                        act.wait_ge(dve_done["score"], 8 * UNITS)
                    op = copy(gate_b[:, e % 2, :], ps[:, :])
                elif kind == "up":
                    b, c = g
                    e, k = divmod(c, KC)
                    o = act_count[st] - 1
                    act.activation(ps[:, :], ps[:, :], ACT.Gelu, bias=vec[:, B1 + c:B1 + c + 1]).then_inc(act_done["gelu"], 1)
                    if o >= FFN_BUFS:
                        act.wait_ge(filled["down"], o - FFN_BUFS + 1)
                    else:
                        act.wait_ge(filled["score"], 8 * UNITS)
                    if dve_splits(b, c):
                        continue
                    act.wait_ge(act_done["gelu"], o + 1)
                    op = copy(ffn_buf(o)[0], ps[:, :])
                elif kind == "store":
                    b, = g
                    out_v = out[b].rearrange("(t p) c -> p t c", p=P)
                    act.wait_ge(dve_done["store"], 2 * b + 1)
                    act.dma_start(out_v[:, 0:2, :], out_tok[:, 0:2, :]).then_inc(stored, 16)
                    act.wait_ge(dve_done["store"], 2 * b + 2)
                    act.dma_start(out_v[:, 2:4, :], out_tok[:, 2:4, :]).then_inc(stored, 16)
                    continue
                else:
                    continue
                op.then_inc(act_done[kind], 1)

            act.wait_ge(stored, 32 * B)

        @block.vector
        def _(dve):
            links = [2]

            def then(op):
                op.then_inc(dve_done["link"], 1)
                links[0] += 1
                dve.wait_ge(dve_done["link"], links[0])

            def token_stats(src):
                for t in range(NT):
                    last = dve.bn_stats(stats[:, t, :], src[:, t, :])
                then(last)
                for t in range(NT):
                    last = dve.bn_aggr(mv[:, t, :], stats[:, t, :])
                return last

            def normalise(dst, src, col, tiles=range(NT)):
                for t in tiles:
                    last = dve.tensor_scalar(dst[:, t, :], src[:, t, :], mv[:, t, 0:1], small[:, col + t:col + t + 1],
                                             ALU.subtract, ALU.mult)
                return last

            dve.memset(o_sb[:, 0, 0:P], 0.0).then_inc(dve_done["link"], 1)
            dve.memset(b2[:, :], 0.0)
            dve.memset(gates_hl[:, :, :], 0.0).then_inc(dve_done["link"], 1)
            for st in DVE_STEPS:
                kind, g = st
                if kind in LAST_READER and LAST_READER[kind] == "dve":
                    ps = bank(st)
                    if kind == "up":
                        pass
                    elif kind in ACT_KINDS and kind != "score":
                        dve.wait_ge(act_done[kind], act_count[st])
                    else:
                        dve.wait_ge(filled[kind], pe_count[st])
                if kind == "xT":
                    b, = g
                    at = slice(b * N, (b + 1) * N)
                    dve.tensor_tensor(xT_lo[:, at], ps[:, :], xT_hi[:, at].bitcast(F32), ALU.subtract)\
                       .then_inc(dve_done["xT"], 1)
                    continue
                elif kind == "split_wqkv" and g[0] in (0, 2):
                    n, = g
                    at = slice(n * 512, (n + 1) * 512)
                    dve.wait_ge(act_done["split_wqkv"], act_count[st])
                    op = dve.tensor_tensor(wq_lo[:, at], stage[:, at], wq_hi[:, at].bitcast(F32), ALU.subtract)
                elif kind in ("projQ", "projK"):
                    u, = g
                    hi, lo, scale = (q_hi, q_lo, SCALE) if kind == "projQ" else (k_hi, k_lo, 1.0)
                    op = dve.scalar_tensor_tensor(lo[:, u % 2, :], ps[:, :], scale, hi[:, u % 2, :].bitcast(F32),
                                                  ALU.mult, ALU.subtract)
                elif kind == "V":
                    b, half, t = g
                    hs = slice(8 * half, 8 * half + 8)
                    op = dve.tensor_tensor(v_hl[:, t, hs, DH:2 * DH], ps[:, :].rearrange("p (h d) -> p h d", d=DH),
                                           v_hl[:, t, hs, 0:DH].bitcast(F32), ALU.subtract)
                elif kind == "score":
                    u, i, j = g
                    s, w = u % 2, P * (i + 1)
                    at = j * HEAD_COLS + ROW_AT[i]
                    dve.wait_ge(pool_done["alibi"], u + 1)
                    if u >= 2:
                        dve.wait_ge(filled["probT"], 6 * (u - 1))
                    op = dve.tensor_tensor_reduce(out=prob[:, s, at:at + w], in0=ps[:, 0:w],
                                                  in1=bias[:, 2 * s + j, N - w:N], scale=-1.0, scalar=BIG,
                                                  op0=ALU.add, op1=ALU.min,
                                                  accum_out=negmax[:, s, 2 * i + j:2 * i + j + 1])
                elif kind == "recip":
                    u, i = g
                    s = u % 2
                    dve.wait_ge(act_done["score"], all_of(act_count, "score", [(u, i, j) for j in range(2)]))
                    op = dve.reciprocal(recip[:, s, 2 * i:2 * i + 2], expsum[:, s, 2 * i:2 * i + 2])
                elif kind == "norm":
                    u, i = g
                    s = u % 2
                    dve.wait_ge(dve_done["recip"], dve_count[("recip", g)])
                    for j in range(2):
                        w = P * (i + 1)
                        at = j * HEAD_COLS + ROW_AT[i]
                        op = dve.tensor_scalar(prob[:, s, at:at + w], prob[:, s, at:at + w],
                                               recip[:, s, 2 * i + j:2 * i + j + 1], None, ALU.mult)
                elif kind == "split_ffn":
                    w, = g
                    both = slice(ffn_w(w)[0], ffn_w(w)[0] + 2 * HID)
                    dve.wait_ge(ffn_loaded[w % FFN_SLOTS], 32 * (w // FFN_SLOTS + 1))
                    if w < FFN_SLOTS:
                        dve.wait_ge(filled["projK"], UNITS)
                        dve.wait_ge(filled["V"], 8 * B)
                    else:
                        dve.wait_ge(filled["down"], KC * (w - FFN_SLOTS + 1))
                    op = dve.tensor_copy(wq_hi[:, both], stage[:, both])
                elif kind == "cols":
                    op = dve.tensor_copy(vec[:, :], ps[:, 0:NROWS])
                elif kind == "ctxV":
                    for b in range(B):
                        op = dve.tensor_tensor(ctx_v[:, b, :], ps[0:S2, b * C:(b + 1) * C], bv_row[:, :], ALU.add)
                    op.then_inc(dve_done["ctxV"], 1)
                    dve.wait_ge(loaded["tail"], 16 * 8)
                    dve.tensor_scalar(keep[:, :, :], mask_i[:, :, :], 0.0, None, ALU.not_equal)\
                       .then_inc(dve_done["mask"], 1)
                    dve.wait_ge(dve_done["mask"], 1)
                    dve.tensor_copy(pick[:, :], pick_f)
                    dve.tensor_scalar(shut[:, :, :], keep[:, :, :], 1.0, NEG, ALU.subtract, ALU.mult)\
                       .then_inc(dve_done["mask"], 1)
                    dve.wait_ge(dve_done["mask"], 2)
                    continue
                elif kind == "probT":
                    u, j, grp = g
                    w = 256 if grp == 2 else 512
                    at = j * HEAD_COLS + GROUP_AT[grp]
                    op = dve.tensor_tensor(pT_lo[:, at:at + w], ps[:, 0:w], pT_hi[:, at:at + w].bitcast(F32),
                                           ALU.subtract)
                elif kind == "res1":
                    b, = g
                    then(dve.tensor_tensor(r_tok[:, :, :], ps[:, :].rearrange("p (t c) -> p t c", t=NT),
                                           x_tok[:, b * NT:(b + 1) * NT, :], ALU.add))
                    op = token_stats(r_tok)
                elif kind == "x1":
                    b, = g
                    dve.wait_ge(pool_done["res1"], b + 1)
                    op = normalise(x1_tok, r_tok, 4)
                elif kind == "xscore":
                    b, = g
                    for t in range(NT):
                        last = dve.scalar_tensor_tensor(xs[:, t, :], ps[:, t * P:t * P + S2], XSCALE, keep[:, b, :],
                                                        ALU.mult, ALU.mult)
                    then(last)
                    then(dve.tensor_tensor(xs[:, :, :], xs[:, :, :],
                                           shut[:, b, :].unsqueeze(1).to_broadcast([P, NT, S2]), ALU.add))
                    then(dve.tensor_reduce(small[:, 8:12], xs[:, :, :], AXIS.X, ALU.max))
                    op = dve.tensor_tensor(xs[:, :, :], xs[:, :, :],
                                           small[:, 8:12].unsqueeze(2).to_broadcast([P, NT, S2]), ALU.subtract)
                elif kind == "xprob":
                    b, = g
                    dve.wait_ge(act_done["xexp"], b + 1)
                    then(dve.tensor_reduce(small[:, 12:16], xs[:, :, :], AXIS.X, ALU.add))
                    then(dve.reciprocal(small[:, 16:20], small[:, 12:16]))
                    op = dve.tensor_tensor(xs[:, :, :], xs[:, :, :],
                                           small[:, 16:20].unsqueeze(2).to_broadcast([P, NT, S2]), ALU.mult)
                elif kind == "xout":
                    b, = g
                    then(dve.tensor_tensor(r_tok[:, :, :], ps[:, :].rearrange("p (t c) -> p t c", t=NT),
                                           x1_tok[:, :, :], ALU.add))
                    op = token_stats(r_tok)
                elif kind == "x2":
                    b, = g
                    dve.wait_ge(pool_done["xout"], b + 1)
                    x2b = x2_tok[:, b * NT:(b + 1) * NT, :]
                    normalise(x2b, r_tok, 20).then_inc(dve_done["x2"], 1)
                    dve.wait_ge(dve_done["x2"], 2 * b + 1)
                    sq = qx_sb[:, :].rearrange("p (t c) -> p t c", t=NT)
                    then(dve.tensor_tensor(sq, x2b, x2b, ALU.mult))
                    op = dve.tensor_reduce(small[:, 24:28], sq, AXIS.X, ALU.add)
                elif kind == "xr":
                    b, = g
                    dve.wait_ge(pool_done["x2"], b + 1)
                    for t in range(NT):
                        op = dve.tensor_scalar(xr_tok[:, t, :], x2_tok[:, b * NT + t, :], small[:, 28 + t:29 + t], None,
                                               ALU.mult)
                elif kind == "xnT":
                    b, = g
                    for e in range(2):
                        hi, lo = xn(b, e)
                        op = dve.scalar_tensor_tensor(lo, ps[:, :], vec[:, GS + e:GS + e + 1], hi.bitcast(F32),
                                                      ALU.mult, ALU.subtract)
                elif kind == "gates":
                    b, = g
                    dve.wait_ge(act_done["logit"], b + 1)
                    flat = sg[:, :, :].rearrange("p t e -> p (t e)")
                    then(dve.tensor_scalar(gates[:, :, :], ez[:, :, :], 1.0, None, ALU.add))
                    then(dve.reciprocal(sg[:, :, :], gates[:, :, :]))
                    c1 = cmp1[:, :, :].rearrange("p (t e) j -> p t e j", t=NT)
                    c2 = cmp2[:, :, :].rearrange("p (t e) j -> p t e j", t=NT)
                    other = sg[:, :, :].unsqueeze(2).to_broadcast([P, NT, ER, ER])
                    own = sg[:, :, :].unsqueeze(3).to_broadcast([P, NT, ER, ER])
                    before = earlier[:, :].unsqueeze(1).to_broadcast([P, NT, ER * ER])
                    dve.tensor_tensor(c1, other, own, ALU.is_gt)
                    then(dve.tensor_tensor(c2, other, own, ALU.is_equal))
                    c2f = cmp2[:, :, :].rearrange("p (t e) j -> p t (e j)", t=NT)
                    then(dve.tensor_tensor(c2f, c2f, before, ALU.mult))
                    then(dve.tensor_tensor(cmp1[:, :, :], cmp1[:, :, :], cmp2[:, :, :], ALU.add))
                    then(dve.tensor_reduce(gates[:, :, :].rearrange("p t e -> p (t e)"), cmp1[:, :, :], AXIS.X, ALU.add))
                    then(dve.tensor_reduce(small[:, 32:36], sg[:, :, :], AXIS.X, ALU.add))
                    dve.reciprocal(small[:, 36:40], small[:, 32:36])
                    then(dve.tensor_scalar(gates[:, :, :], gates[:, :, :], 1.5, None, ALU.is_lt))
                    then(dve.tensor_tensor(gates[:, :, :], gates[:, :, :], sg[:, :, :], ALU.mult))
                    then(dve.tensor_tensor(gates[:, :, :], gates[:, :, :],
                                           small[:, 36:40].unsqueeze(2).to_broadcast([P, NT, ER]), ALU.mult))
                    then(dve.tensor_copy(g_hi[:, :, :], gates[:, :, :]))
                    dve.tensor_copy(gates_hl[:, :, ES:E], g_hi[:, :, :].bitcast(F32))
                    dve.memset(gates_hl[:, :, 0:ES], 1.0)
                    op = dve.tensor_tensor(gates_hl[:, :, 16 + ES:16 + E], gates[:, :, :], g_hi[:, :, :].bitcast(F32),
                                           ALU.subtract)
                elif kind == "up":
                    b, c = g
                    n = b * CHUNKS + c
                    hi, lo = ffn_buf(n)
                    if dve_splits(b, c):
                        if n >= FFN_BUFS:
                            dve.wait_ge(filled["down"], n - FFN_BUFS + 1)
                        else:
                            dve.wait_ge(filled["score"], 8 * UNITS)
                        dve.wait_ge(act_done["gelu"], n + 1)
                        then(dve.tensor_copy(hi, ps[:, :]))
                    else:
                        dve.wait_ge(act_done["up"], up_copies[(b, c)])
                    op = dve.tensor_tensor(lo, ps[:, :], hi.bitcast(F32), ALU.subtract)
                elif kind == "gated":
                    b, e = g
                    m = y_index(b, e)
                    dve.wait_ge(filled["down"], pe_count[("down", (b, e * KC + KC - 1))])
                    if e < ES:
                        op = dve.tensor_copy(acc[:, b * N:(b + 1) * N], sum_bank[m % 2][:, :])
                    else:
                        i = b * ER + e - ES
                        dve.wait_ge(act_done["gate_b"], i + 1)
                        if i >= 2 and (i - 1) % ER:
                            dve.wait_ge(pool_done["gated"], pool_adds(i - 1))
                        elif i >= 2:
                            dve.wait_ge(filled["final"], (i - 1) // ER)
                        op = dve.tensor_tensor(part[:, (i % 2) * N:(i % 2 + 1) * N], sum_bank[m % 2][:, :],
                                               gate_b[:, e % 2, :], ALU.mult)
                elif kind == "most":
                    b, = g
                    if b == 1:
                        dve.wait_ge(stored, 32)
                    flat = x2_tok[:, b * NT:(b + 1) * NT, :].rearrange("p t c -> p (t c)")
                    op = dve.scalar_tensor_tensor(r_tok[:, :, :].rearrange("p t c -> p (t c)"), flat, 2.0, ps[:, :],
                                                  ALU.mult, ALU.add)
                elif kind == "final":
                    b, = g
                    dve.wait_ge(dve_done["most"], b + 1)
                    then(dve.tensor_tensor(r_tok[:, :, :].rearrange("p t c -> p (t c)"),
                                           r_tok[:, :, :].rearrange("p t c -> p (t c)"), ps[:, :], ALU.add))
                    op = token_stats(r_tok)
                elif kind == "store":
                    b, = g
                    dve.wait_ge(pool_done["final"], b + 1)
                    normalise(out_tok, r_tok, 40, (0, 1)).then_inc(dve_done["store"], 1)
                    op = normalise(out_tok, r_tok, 40, (2, 3))
                else:
                    continue
                op.then_inc(dve_done[kind], 1)

        @block.gpsimd
        def _(pool):
            links = [0]

            def then(op):
                op.then_inc(pool_done["pool_link"], 1)
                links[0] += 1
                pool.wait_ge(pool_done["pool_link"], links[0])

            def power(dst, src, scale, eps):
                then(pool.tensor_scalar(small[:, dst:dst + NT], src, scale, eps, ALU.mult, ALU.add))
                return pool.tensor_tensor(small[:, dst:dst + NT], small[:, dst:dst + NT], small[:, 0:NT], ALU.pow)

            def alibi(u):
                for j in range(2):
                    last = pool.tensor_scalar(bias[:, 2 * (u % 2) + j, :], rel[:, :], SLOPES[2 * (u % PAIRS) + j], None, ALU.mult)
                last.then_inc(pool_done["alibi"], 1)

            then(pool.memset(small[:, 0:NT], -0.5))
            for st in POOL_STEPS:
                kind, g = st
                if kind == "split_wqkv" and g[0] not in (0, 2):
                    n, = g
                    at = slice(n * 512, (n + 1) * 512)
                    pool.wait_ge(act_done["split_wqkv"], act_count[st])
                    pool.tensor_tensor(wq_lo[:, at], stage[:, at], wq_hi[:, at].bitcast(F32), ALU.subtract)\
                        .then_inc(pool_done["split_wqkv"], 1)
                elif kind == "alibi":
                    u, = g
                    pool.wait_ge(loaded["rel"], 16)
                    if u >= 2:
                        scores = [(u - 2, i, j) for i in range(NT) for j in range(2)]
                        pool.wait_ge(dve_done["score"], all_of(dve_count, "score", scores))
                    alibi(u)
                elif kind == "pool_norm":
                    u, i = g
                    s, w = u % 2, P * (i + 1)
                    pool.wait_ge(dve_done["recip"], dve_count[("recip", g)])
                    for j in range(2):
                        at = j * HEAD_COLS + ROW_AT[i]
                        op = pool.tensor_scalar(prob[:, s, at:at + w], prob[:, s, at:at + w],
                                                recip[:, s, 2 * i + j:2 * i + j + 1], None, ALU.mult)
                    op.then_inc(pool_done["pool_norm"], 1)
                elif kind == "split_ffn":
                    w, = g
                    both = slice(ffn_w(w)[0], ffn_w(w)[0] + 2 * HID)
                    pool.wait_ge(dve_done["split_ffn"], w + 1)
                    pool.tensor_tensor(wq_lo[:, both], stage[:, both], wq_hi[:, both].bitcast(F32), ALU.subtract)\
                        .then_inc(pool_done["split_ffn"], 1)
                elif kind == "res1":
                    b, = g
                    pool.wait_ge(dve_done["res1"], b + 1)
                    power(4, mv[:, :, 1], 1.0, LN_EPS).then_inc(pool_done["res1"], 1)
                elif kind == "xout":
                    b, = g
                    pool.wait_ge(dve_done["xout"], b + 1)
                    power(20, mv[:, :, 1], 1.0, LN_EPS).then_inc(pool_done["xout"], 1)
                elif kind == "x2":
                    b, = g
                    pool.wait_ge(dve_done["x2"], 2 * b + 2)
                    power(28, small[:, 24:28], 1.0 / C, RMS_EPS).then_inc(pool_done["x2"], 1)
                elif kind == "gated" and ES <= g[1] < E - 1:
                    b, e = g
                    i = b * ER + e - ES
                    pool.wait_ge(dve_done["gated"], y_index(b, e) + 1)
                    if i:
                        pool.wait_ge(pool_done["gated"], pool_adds(i))
                    pool.tensor_tensor(acc[:, b * N:(b + 1) * N], acc[:, b * N:(b + 1) * N],
                                       part[:, (i % 2) * N:(i % 2 + 1) * N], ALU.add).then_inc(pool_done["gated"], 1)
                elif kind == "final":
                    b, = g
                    pool.wait_ge(dve_done["final"], b + 1)
                    power(40, mv[:, :, 1], 1.0, LN_EPS).then_inc(pool_done["final"], 1)


_INS = ['x', 'ctx_1024', 'mask_BxS2_if1', 'L0_attn_w_qkv', 'L0_attn_w_out', 'L0_attn_b_out', 'L0_xattn_Wq',
        'L0_xattn_bq', 'L0_xattn_Wk', 'L0_xattn_bk', 'L0_xattn_Wv', 'L0_xattn_bv', 'L0_ffn_g_shared', 'L0_ffn_W1_s',
        'L0_ffn_b1_s', 'L0_ffn_W2_s', 'L0_ffn_b2_s', 'L0_ffn_g_routed', 'L0_ffn_W1_r', 'L0_ffn_b1_r', 'L0_ffn_W2_r',
        'L0_ffn_b2_r', 'L0_ffn_centroids']


def shape_constants():
    import numpy as np
    p, c = np.arange(P)[:, None], np.arange(N)[None, :]
    rel = (c - p - (N - P)).astype(np.float32)
    rel = np.where(rel > 0, np.float32(-NEG * 100), rel).astype(np.float32)
    e = np.arange(ER)
    earlier = np.broadcast_to((e[None, :] < e[:, None]).astype(np.float32).reshape(1, -1), (P, ER * ER))
    pick = np.zeros((32, ER, P), np.float32)
    for k in range(ER):
        pick[ES + k, k] = pick[16 + ES + k, k] = 1.0
    return {"rel": rel, "ident": np.eye(P, dtype=np.float32), "earlier": np.ascontiguousarray(earlier),
            "pick": pick.reshape(32, ER * P)}


def kernel(**inputs):
    import numpy as np
    import concourse.bacc as bacc
    from concourse import mybir as mb
    from concourse.bass_utils import run_bass_kernel_spmd

    nc = bacc.Bacc("TRN2", target_bir_lowering=False, num_devices=1)
    arrays, aps = {}, {}
    for name, arr in [(n, inputs[n]) for n in _INS] + list(shape_constants().items()):
        arr = np.ascontiguousarray(arr)
        arrays[f"in_{name}"] = arr
        aps[name] = nc.dram_tensor(f"in_{name}", arr.shape, mb.dt.from_np(arr.dtype), kind="ExternalInput").ap()
    out = nc.dram_tensor("out_dram", (B, N, C), mb.dt.float32, kind="ExternalOutput").ap()
    decoder_block(nc, aps, out)
    r = run_bass_kernel_spmd(nc, [arrays], core_ids=[0])
    return r.results[0]["out_dram"]
```
